# Optimizing a Trainium2 kernel written in Bass

```python
import numpy as np
import jax
import jax.numpy as jnp

def _softmax(x, axis=-1):
    return jax.nn.softmax(x, axis=axis)

def _gelu(x):
    return jax.nn.gelu(x, approximate=True)

def _silu(x):
    return jax.nn.silu(x)

def _sigmoid(x):
    return jax.nn.sigmoid(x)

def _layernorm(x, axis=-1, eps=1e-05):
    m = jnp.mean(x, axis=axis, keepdims=True)
    v = jnp.var(x, axis=axis, keepdims=True)
    return (x - m) / jnp.sqrt(v + eps)

def _scatter_add(tgt, idx, src, axis=0):
    return tgt.at[idx].add(src)

def _segment_sum(src, seg, n):
    return jax.ops.segment_sum(src, seg, n)
kernel_name = 'mk_adj_preln_d2_adj_r2_f254b9'

def setup_inputs(seed: int=0):
    np.random.seed(seed)
    _w = jnp.asarray

    def _rec_inputs():
        import jax
        import jax.numpy as jnp
        _gk = jax.random.key(seed)
        x = -0.0005207 + 1.001 * jax.random.normal(jax.random.fold_in(_gk, 1), (2048, 256), jnp.float32)
        _a = jax.random.bernoulli(jax.random.fold_in(_gk, 2), 0.00195312, (2048, 2048))
        _a = jnp.logical_or(_a, jnp.eye(2048, dtype=bool))
        _af = _a.astype(jnp.float32)
        _af = _af * jax.random.uniform(jax.random.fold_in(_gk, 3), (2048, 2048), jnp.float32, 0.05, 1)
        adj = _af
        return (x, adj)
    x, adj = _rec_inputs()

    def _L0_gnn_setup():
        import jax, jax.numpy as jnp
        import numpy as np
        N, D_IN, D_ATTN, STEPS, P_NUC, TAU = (2048, 256, 64, 2, 0.9, 1.0)
        LN_EPS = 1e-05

        def _xavier(key, shape):
            fan_in, fan_out = (shape[-2], shape[-1])
            lim = np.sqrt(6.0 / (fan_in + fan_out))
            return jax.random.uniform(key, shape, jnp.float32, -lim, lim)

        def _adj_from_feats(Xa, W1, W2, W3):
            Q = Xa @ W1
            K = Xa @ W3
            logits = Q @ W2 @ K.T / TAU
            idx = jnp.argsort(-logits, axis=1)
            vals = jnp.take_along_axis(logits, idx, axis=1)
            csum = jnp.cumsum(jax.nn.softmax(vals, axis=1), axis=1)
            k_i = jnp.sum(csum < P_NUC, axis=1) + 1
            ranks = jnp.arange(logits.shape[1])[None, :]
            keep_sorted = ranks < k_i[:, None]
            inv = jnp.argsort(idx, axis=1)
            keep = jnp.take_along_axis(keep_sorted, inv, axis=1)
            masked = jnp.where(keep, logits, -jnp.inf)
            return jax.nn.softmax(masked, axis=1)
        key = jax.random.key(seed)
        ks = jax.random.split(key, 9)
        return {'X': jax.random.normal(ks[0], (N, D_IN), jnp.float32), 'S': jax.random.uniform(ks[1], (N, N), jnp.float32), 'W1': _xavier(ks[2], (D_IN, D_ATTN)), 'W2': _xavier(ks[3], (D_ATTN, D_ATTN)), 'W3': _xavier(ks[4], (D_IN, D_ATTN)), 'U1': _xavier(ks[5], (STEPS, D_IN, D_IN)), 'U2': _xavier(ks[6], (STEPS, D_IN, D_IN)), 'U3': _xavier(ks[7], (STEPS, D_IN, D_IN)), 'gamma': jnp.ones((D_IN,), jnp.float32), 'beta': jnp.zeros((D_IN,), jnp.float32)}
    _L0_gnn_all = _L0_gnn_setup()
    _L0_gnn_in = {k: v for k, v in _L0_gnn_all.items() if k in ('W1', 'W2', 'W3', 'U1', 'U2', 'U3', 'gamma', 'beta')}
    del _L0_gnn_all

    def _L1_gnn_setup():
        import jax, jax.numpy as jnp
        import numpy as np
        N = 3072
        D_IN = 256
        D_OUT = 256
        DENSITY = 0.005
        key = jax.random.key(seed)
        ks = jax.random.split(key, 12)
        x = jax.random.normal(ks[0], (N, D_IN), dtype=jnp.float32)
        adj_a = (jax.random.uniform(ks[1], (N, N)) < DENSITY).astype(jnp.float32)
        adj_b = (jax.random.uniform(ks[2], (N, N)) < DENSITY).astype(jnp.float32)
        W_sa = jax.random.normal(ks[3], (D_IN, D_OUT), dtype=jnp.float32) * (1.414 / np.sqrt(D_IN + D_OUT))
        a_sa = jax.random.normal(ks[4], (1, 2 * D_OUT), dtype=jnp.float32) * (1.414 / np.sqrt(1 + 2 * D_OUT))
        stdv = 1.0 / np.sqrt(D_OUT)
        W_gcnb = jax.random.uniform(ks[5], (D_IN, D_OUT), minval=-stdv, maxval=stdv, dtype=jnp.float32)
        b_gcnb = jax.random.uniform(ks[6], (D_OUT,), minval=-stdv, maxval=stdv, dtype=jnp.float32)
        s = 1.0 / np.sqrt(2 * D_IN)
        Wa = jax.random.uniform(ks[7], (1, 2 * D_IN), minval=-s, maxval=s, dtype=jnp.float32)
        ba = jax.random.uniform(ks[8], (1,), minval=-s, maxval=s, dtype=jnp.float32)
        Wb = jax.random.uniform(ks[9], (1, 2 * D_IN), minval=-s, maxval=s, dtype=jnp.float32)
        bb = jax.random.uniform(ks[10], (1,), minval=-s, maxval=s, dtype=jnp.float32)
        return {'x': x, 'adj_a': adj_a, 'adj_b': adj_b, 'W_sa': W_sa, 'a_sa': a_sa, 'W_gcnb': W_gcnb, 'b_gcnb': b_gcnb, 'Wa': Wa, 'ba': ba, 'Wb': Wb, 'bb': bb}
    _L1_gnn_all = _L1_gnn_setup()
    _L1_gnn_in = {k: v for k, v in _L1_gnn_all.items() if k in ('W_sa', 'a_sa', 'W_gcnb', 'b_gcnb', 'Wa', 'ba', 'Wb', 'bb')}
    del _L1_gnn_all
    return {'x': x, 'adj': adj, 'L0_gnn_W1': _L0_gnn_in['W1'], 'L0_gnn_W2': _L0_gnn_in['W2'], 'L0_gnn_W3': _L0_gnn_in['W3'], 'L0_gnn_U1': _L0_gnn_in['U1'], 'L0_gnn_U2': _L0_gnn_in['U2'], 'L0_gnn_U3': _L0_gnn_in['U3'], 'L0_gnn_gamma': _L0_gnn_in['gamma'], 'L0_gnn_beta': _L0_gnn_in['beta'], 'L1_gnn_W_sa': _L1_gnn_in['W_sa'], 'L1_gnn_a_sa': _L1_gnn_in['a_sa'], 'L1_gnn_W_gcnb': _L1_gnn_in['W_gcnb'], 'L1_gnn_b_gcnb': _L1_gnn_in['b_gcnb'], 'L1_gnn_Wa': _L1_gnn_in['Wa'], 'L1_gnn_ba': _L1_gnn_in['ba'], 'L1_gnn_Wb': _L1_gnn_in['Wb'], 'L1_gnn_bb': _L1_gnn_in['bb']}

def reference(x, adj, L0_gnn_W1, L0_gnn_W2, L0_gnn_W3, L0_gnn_U1, L0_gnn_U2, L0_gnn_U3, L0_gnn_gamma, L0_gnn_beta, L1_gnn_W_sa, L1_gnn_a_sa, L1_gnn_W_gcnb, L1_gnn_b_gcnb, L1_gnn_Wa, L1_gnn_ba, L1_gnn_Wb, L1_gnn_bb):
    import jax
    import jax.numpy as jnp

    def _L0_gnn_ref(X, S, W1, W2, W3, U1, U2, U3, gamma, beta):
        import jax, jax.numpy as jnp
        import numpy as np
        N, D_IN, D_ATTN, STEPS, P_NUC, TAU = (2048, 256, 64, 2, 0.9, 1.0)
        LN_EPS = 1e-05

        def _xavier(key, shape):
            fan_in, fan_out = (shape[-2], shape[-1])
            lim = np.sqrt(6.0 / (fan_in + fan_out))
            return jax.random.uniform(key, shape, jnp.float32, -lim, lim)

        def _adj_from_feats(Xa, W1, W2, W3):
            Q = Xa @ W1
            K = Xa @ W3
            logits = Q @ W2 @ K.T / TAU
            idx = jnp.argsort(-logits, axis=1)
            vals = jnp.take_along_axis(logits, idx, axis=1)
            csum = jnp.cumsum(jax.nn.softmax(vals, axis=1), axis=1)
            k_i = jnp.sum(csum < P_NUC, axis=1) + 1
            ranks = jnp.arange(logits.shape[1])[None, :]
            keep_sorted = ranks < k_i[:, None]
            inv = jnp.argsort(idx, axis=1)
            keep = jnp.take_along_axis(keep_sorted, inv, axis=1)
            masked = jnp.where(keep, logits, -jnp.inf)
            return jax.nn.softmax(masked, axis=1)
        n = X.shape[0]
        S = S + jnp.eye(n, dtype=X.dtype)
        Rf = S / jnp.clip(S.sum(axis=1, keepdims=True), 1e-12)
        Rb = S / jnp.clip(S.sum(axis=0), 1e-12)[:, None]
        Xf, Xb, Xa = (X, X, X)
        Z = jnp.zeros_like(X)
        for s in range(STEPS):
            A = _adj_from_feats(Xa, W1, W2, W3)
            Xf = Rf @ Xf
            Xb = Rb @ Xb
            Xa = A @ Xa
            Z = Z + (Xf @ U1[s] + Xb @ U2[s] + Xa @ U3[s])
        Y = X + Z
        mu = Y.mean(axis=-1, keepdims=True)
        var = Y.var(axis=-1, keepdims=True)
        return (Y - mu) / jnp.sqrt(var + LN_EPS) * gamma + beta

    def _L1_gnn_ref(x, adj_a, adj_b, W_sa, a_sa, W_gcnb, b_gcnb, Wa, ba, Wb, bb):
        import jax, jax.numpy as jnp
        import numpy as np
        N = 3072
        D_IN = 256
        D_OUT = 256
        DENSITY = 0.005
        type_sum_a = adj_a @ x
        type_sum_b = adj_b @ x
        attn_a = jax.nn.sigmoid(jnp.concatenate([type_sum_a, x], axis=1) @ Wa.T + ba)
        attn_b = jax.nn.sigmoid(jnp.concatenate([type_sum_b, x], axis=1) @ Wb.T + bb)
        h = x @ W_sa
        Hd = h.shape[1]
        s_left = h @ a_sa[0, :Hd]
        s_right = h @ a_sa[0, Hd:]
        scores = s_left[:, None] + s_right[None, :]
        e = jnp.where(adj_a != 0, jnp.exp(-jax.nn.leaky_relu(scores, 0.01)), 0.0)
        attn = e / (jnp.sum(e, axis=1, keepdims=True) + 1e-05)
        x_a = attn @ h
        x_b = adj_b @ (x @ W_gcnb) + b_gcnb
        return jax.nn.sigmoid(attn_a * x_a + attn_b * x_b)
    h = jnp.maximum(_layernorm(x, axis=-1), 0.0)
    x = x + _L0_gnn_ref(h, adj, L0_gnn_W1, L0_gnn_W2, L0_gnn_W3, L0_gnn_U1, L0_gnn_U2, L0_gnn_U3, L0_gnn_gamma, L0_gnn_beta)
    h = jnp.maximum(_layernorm(x, axis=-1), 0.0)
    x = x + _L1_gnn_ref(h, adj, adj, L1_gnn_W_sa, L1_gnn_a_sa, L1_gnn_W_gcnb, L1_gnn_b_gcnb, L1_gnn_Wa, L1_gnn_ba, L1_gnn_Wb, L1_gnn_bb)
    return x

_drawn_inputs = setup_inputs


def setup_inputs(seed=0):
    import zlib

    import numpy as np

    out = dict(_drawn_inputs(seed))
    spreads = {'L0_gnn_gamma': (1.0, 0.2), 'L0_gnn_beta': (0.0, 0.1)}
    factors = {'L1_gnn_a_sa': 8.0, 'L1_gnn_b_gcnb': 8.0, 'L1_gnn_Wa': 8.0, 'L1_gnn_Wb': 3.602}
    for name, (base, spread) in spreads.items():
        noise = np.random.default_rng([zlib.crc32(name.encode()), seed]).standard_normal(out[name].shape)
        drawn = base * np.exp(spread * noise) if base else spread * noise
        out[name] = jnp.asarray(drawn.astype(out[name].dtype))
    for name, factor in factors.items():
        out[name] = (out[name] * factor).astype(out[name].dtype)
    return out
```

```python
import math

import numpy as np

import concourse.bass as bass
from concourse import mybir
from contextlib import ExitStack


def gnn_block_program(nc, x_d, adjt_d, w1t_d, w2_d, w3_d, u1_d, u2_d, u3_d, gamma_d, beta_d,
                      wsa_d, asa_d, wg_d, bg_d, wgate_d, ba_d, bb_d, ident_d, out_d):
    F32 = mybir.dt.float32
    F16 = mybir.dt.float16
    ALU = mybir.AluOpType
    ACT = mybir.ActivationFunctionType
    AX = mybir.AxisListType

    P = 128
    N, D = x_d.shape
    NT = N // P
    KD = D // P
    DA = w2_d.shape[0]
    NP = NT // 2
    CH = 512
    NCH = N // CH
    LN_EPS = 1e-5
    P_NUC = 0.9
    SQK = 64.0
    LSCALE = 1.0 / (SQK * SQK)
    FLOOR = (1.0 - P_NUC) / N
    WIDTH = -math.log(FLOOR)
    PASSES = 22

    ctx = ExitStack()
    with ctx:
        def sb(name, shape, dt=F32):
            return ctx.enter_context(nc.sbuf_tensor(name, shape, dt))

        def ps(name, shape):
            return ctx.enter_context(nc.psum_tensor(name, shape, F32))

        def some(count):
            return not isinstance(count, int) or count > 0

        def sem(name):
            return ctx.enter_context(nc.semaphore(name))

        ident = sb("ident", [P, P])
        ones = sb("ones", [P, P])
        w1t = sb("w1t", [DA, D])
        w22 = sb("w22", [DA, 2 * DA])
        w33 = sb("w33", [P, KD, 2 * DA])
        w12 = sb("w12", [P, KD, 2 * DA])
        u12a = sb("u12a", [P, KD, 2 * D])
        u12b = sb("u12b", [P, KD, 2 * D])
        u3 = sb("u3", [P, KD, 2 * D])
        gamma = sb("gamma", [P, D])
        beta = sb("beta", [P, D])
        wsg = sb("wsg", [P, KD, D + 4])
        wg = sb("wg", [P, KD, D])
        asa = sb("asa", [P, 2 * D])
        bg = sb("bg", [P, D])
        bab = sb("bab", [P, 2])

        xc = sb("xc", [P, NT, D + 2])
        xt = sb("xt", [P, KD, N])
        qs = sb("qs", [P, N], F16)
        kh = sb("kh", [P, N], F16)
        kl = sb("kl", [P, N], F16)
        ew = sb("ew", [P, 2, N])
        em = sb("em", [P, N])
        emt = sb("emt", [P, NT, P])
        adjb = sb("adjb", [P, 2, N])
        cacc = sb("cacc", [P, NT, P // 2])
        pst = sb("pst", [P, D + 1])
        pair_t = sb("pair_t", [P, 2, KD, P])
        ptt = pair_t[:, 0, :, :]
        xst = sb("xst", [P, D])
        xtt = pair_t[:, 1, :, :]
        z = sb("z", [P, NT, D])
        pu2 = sb("pu2", [P, NT, D])
        g = sb("g", [P, NT, 2 * D])
        r3 = sb("r3", [P, NT, D])
        stats = sb("stats", [P, NT, 6])
        mv = sb("mv", [P, NT, 2])
        rstd = sb("rstd", [P, NT])
        nmr = sb("nmr", [P, NT])
        tn = sb("tn", [P, NT])
        half = sb("half", [P, NT])
        rinv = sb("rinv", [P, NT])
        cinv = sb("cinv", [P, NT])
        nmax = sb("nmax", [P, 2])
        nbias = sb("nbias", [P, 2])
        zsum = sb("zsum", [P, 2])
        target = sb("target", [P, 1])
        lo = sb("lo", [P, 1])
        probe = sb("probe", [P, 1])
        hit = sb("hit", [P, 1])
        mass = sb("mass", [P, 1])
        den = sb("den", [P, 1])
        dinv = sb("dinv", [P, 2])
        junk = em[:, 0:N // 2].bitcast(F16)
        w = pair_t[:, :, :, :].rearrange("p a k n -> p (a k n)")
        sl = sb("sl", [P, NT])
        sr = sb("sr", [P, NT])
        ga = sb("ga", [P, NT, 2])
        gz = sb("gz", [P, 2])
        ge = sb("ge", [P, 2])
        fe = u12a[:, 0, :].rearrange("p (a n) -> p a n", a=2)
        fin = u12a[:, 1, :].rearrange("p (a n) -> p a n", a=2)

        pL = ps("pL", [P, N])
        pT = [ps("pT0", [P, CH]), ps("pT1", [P, CH])]
        pS = ps("pS", [P, CH])
        pA = ps("pA", [P, CH])

        s_wts = sem("weights_loaded")
        s_x = sem("x_loaded")
        s_x2 = sem("x_loaded_again")
        s_adj = [sem("adj_loaded0"), sem("adj_loaded1")]
        s_adjf = [sem("adj_used0"), sem("adj_used1")]
        s_csum = [sem("adj_summed0"), sem("adj_summed1")]
        s_out = sem("out_stored")
        s_dve = sem("dve_chain")
        s_pool = sem("pool_chain")
        s_ms = sem("constants_set")
        s_col = sem("column_of_ones")
        s_var = sem("variance_ready")
        s_pow = sem("rsqrt_guess_ready")
        s_nrm = sem("norm_ready")
        s_xc = sem("x_normed")
        s_w12p = sem("w12_product")
        s_w12 = sem("w12_ready")
        s_tp = [sem("transposed0"), sem("transposed1")]
        s_te = [sem("transpose_copied0"), sem("transpose_copied1")]
        s_xtc = sem("xt_ready")
        s_qp = [sem("qk_product0"), sem("qk_product1")]
        s_qe = [sem("qk_split0"), sem("qk_split1")]
        s_qh = [sem("qk_high0"), sem("qk_high1")]
        s_L = sem("logits_ready")
        s_max = sem("max_ready")
        s_e = sem("exp_ready")
        s_em = sem("kept_ready")
        s_emu = sem("kept_transposed")
        s_et = sem("kept_columns_copied")
        s_A = sem("attention_product")
        s_Ae = sem("attention_copied")
        s_S = sem("adjacency_product")
        s_Se = sem("adjacency_copied")
        s_pt = sem("p_transposed")
        s_ptc = sem("p_columns_copied")
        s_PU = sem("p_u_products")
        s_PUe = sem("p_u_products_read")
        s_at = sem("ax_transposed")
        s_atc = sem("ax_columns_copied")
        s_AU = sem("ax_u3_product")
        s_AUe = sem("ax_u3_product_read")
        s_h1 = sem("h1_ready")
        s_m = sem("h_products")
        s_me = sem("h_products_read")
        s_gs = sem("g_scaled")
        s_dinv = sem("kept_mass_inverted")
        s_diag = sem("diag_ready")
        s_slb = sem("s_left_spread")
        s_slc = sem("s_left_copied")
        s_sco = sem("scores_ready")
        s_lr = sem("leaky_ready")
        s_ex = sem("edge_exp_ready")
        s_mk = sem("edge_weights_ready")
        s_mku = sem("edge_weights_used")
        s_xa = sem("xa_product")
        s_xb = sem("xb_product")
        s_rd = sem("products_read")
        s_gz = sem("gate_logits")
        s_ge = sem("gate_exp")
        s_y = sem("y_ready")
        s_ye = sem("y_exp")
        s_fin = sem("out_tile_ready")

        edge = em
        sco = ew[:, 0, :]
        lrb = ew[:, 1, :]
        slb = g[:, :, :].rearrange("p t n -> p (t n)")[:, NT * 2 * D - N:]
        h257 = g[:, :, :].rearrange("p t n -> p (t n)")[:, 0:NT * (D + 1)].rearrange("p (t n) -> p t n", t=NT)
        xgate = xc

        WTS = 16 * 21

        block = ctx.enter_context(nc.Block())

        @block.sync
        def _(sp):
            sp.dma_start(r3[:, :, :], x_d.rearrange("(t p) n -> p t n", p=P)).then_inc(s_x, 16)
            loads = [(ident[:, :], ident_d), (w1t[:, :], w1t_d),
                     (w22[:, 0:DA], w2_d), (w22[:, DA:2 * DA], w2_d),
                     (w33[:, :, 0:DA], w3_d.rearrange("(k p) n -> p k n", p=P)),
                     (w33[:, :, DA:2 * DA], w3_d.rearrange("(k p) n -> p k n", p=P)),
                     (gamma[:, :], gamma_d.partition_broadcast(P)), (beta[:, :], beta_d.partition_broadcast(P)),
                     (wsg[:, :, 0:D], wsa_d.rearrange("(k p) n -> p k n", p=P)),
                     (wsg[:, :, D:D + 4], wgate_d.rearrange("(k p) n -> p k n", p=P)),
                     (wg[:, :, :], wg_d.rearrange("(k p) n -> p k n", p=P)),
                     (asa[:, :], asa_d.partition_broadcast(P)), (bg[:, :], bg_d.partition_broadcast(P)),
                     (bab[:, 0:1], ba_d.partition_broadcast(P)), (bab[:, 1:2], bb_d.partition_broadcast(P))]
            for s in range(2):
                for dst, c, u_d in ((u12a if s == 0 else u12b, 0, u1_d), (u12a if s == 0 else u12b, 1, u2_d), (u3, s, u3_d)):
                    loads.append((dst[:, :, c * D:(c + 1) * D], u_d[s, :, :].rearrange("(k p) n -> p k n", p=P)))
            for dst, src in loads:
                sp.dma_start(dst, src).then_inc(s_wts, 16)
            assert 16 * len(loads) == WTS

            def adj_pair(sweep, q):
                for b in range(2):
                    if sweep > 0:
                        if some(NP * sweep + q):
                            sp.wait_ge(s_adjf[b], NP * sweep + q)
                    else:
                        if some(q):
                            sp.wait_ge(s_adjf[b], q)
                    if sweep == 0:
                        if some(q):
                            sp.wait_ge(s_csum[b], q)
                    elif sweep == 1 and isinstance(q, int):
                        sp.wait_ge(s_csum[b], NP)
                    sp.dma_start(adjb[:, b, :], adjt_d[bass.ds(2 * q + b, 1), :, :].rearrange("a p n -> p (a n)")
                                 ).then_inc(s_adj[b], 16)

            adj_pair(0, 0)
            with sp.Fori(1, NP) as q:
                adj_pair(0, q)
            adj_pair(1, 0)
            with sp.Fori(1, NP) as q:
                adj_pair(1, q)
            with sp.Fori(0, NP) as q:
                adj_pair(2, q)

        @block.gpsimd
        def _(pool):
            pool.memset(ones[:, :], 1.0).then_inc(s_ms, 1)
            pool.memset(half[:, :], -0.5).then_inc(s_ms, 1)
            pool.memset(cacc[:, :, :], 0.0).then_inc(s_pool, 1)
            pool.wait_ge(s_ms, 2)

            def rsqrt_guess(n):
                pool.wait_ge(s_var, n + 1)
                pool.tensor_tensor(rstd[:, :], tn[:, :], half[:, :], ALU.pow).then_inc(s_pow, 1)

            rsqrt_guess(0)
            with pool.Fori(0, NP) as q:
                for b in range(2):
                    pool.wait_ge(s_adj[b], 16 * q + 16)
                    blk = adjb[:, b, :].rearrange("p (t h i) -> p t h i", h=2, i=P // 2)
                    pool.wait_ge(s_pool, 4 * q + 2 * b + 1)
                    pool.tensor_tensor(cacc[:, :, :], cacc[:, :, :], blk[:, :, 0, :], ALU.add).then_inc(s_pool, 1)
                    pool.wait_ge(s_pool, 4 * q + 2 * b + 2)
                    pool.tensor_tensor(cacc[:, :, :], cacc[:, :, :], blk[:, :, 1, :], ALU.add).then_inc(s_pool, 1)
                    pool.wait_ge(s_pool, 4 * q + 2 * b + 3)
                    pool.nop().then_inc(s_csum[b], 1)
            rsqrt_guess(1)
            pool.wait_ge(s_A, NT)
            pool.wait_ge(s_PUe, NT)
            pool.dma_start(xc[:, :, 0:D], x_d.rearrange("(t p) n -> p t n", p=P)).then_inc(s_x2, 16)
            rsqrt_guess(2)

            pool.wait_ge(s_slc, 1)
            pool.wait_ge(s_me, NT)
            def scores(t):
                if some(t):
                    pool.wait_ge(s_lr, t)
                pool.tensor_tensor(sco.rearrange("p (t i) -> p t i", i=P),
                                   slb[:, bass.ds(t * P, P)].rearrange("p (a i) -> p a i", a=1).to_broadcast([P, NT, P]),
                                   sr[:, :].rearrange("p (t a) -> p t a", a=1).to_broadcast([P, NT, P]),
                                   ALU.add).then_inc(s_sco, 1)

            scores(0)
            with pool.Fori(1, NT) as t:
                scores(t)

        @block.scalar
        def _(act):
            def rows(t):
                return bass.ds(t * P, P)

            act.wait_ge(s_x, 16)
            act.wait_ge(s_nrm, 1)
            for t in range(NT):
                act.activation(xc[:, t, 0:D], r3[:, t, :], ACT.Relu, bias=nmr[:, t:t + 1],
                               scale=rstd[:, t:t + 1]).then_inc(s_xc, 1)
            act.wait_ge(s_w12p, 1)
            act.activation(w12[:, :, :], pS[:, 0:KD * P], ACT.Copy).then_inc(s_w12, 1)

            def xt_copies(s):
                for n in range(KD * NCH):
                    b = n % 2
                    act.wait_ge(s_tp[b], 4 * s + n // 2 + 1)
                    act.activation(xt[:, n % KD, (n // KD) * CH:(n // KD + 1) * CH], pT[b][:, :], ACT.Copy).then_inc(s_te[b], 1)

            def qk_high(s):
                for n in range(NCH):
                    for b, dst in ((0, qs), (1, kh)):
                        act.wait_ge(s_qp[b], NCH * s + n + 1)
                        act.activation(dst[:, n * CH:(n + 1) * CH], pT[b][:, :], ACT.Copy, scale=SQK).then_inc(s_qh[b], 1)

            def exps(s, t, b):
                act.wait_ge(s_max, s * NT + t + 1)
                if s > 0 or not isinstance(t, int) or t >= 2:
                    act.wait_ge(s_em, s * NT + t - 1)
                act.activation(ew[:, b, :], pL[:, :], ACT.Exp, bias=nbias[:, b:b + 1], scale=LSCALE,
                               accum_out=zsum[:, b:b + 1]).then_inc(s_e, 1)

            def tile(s, t, b, more):
                if more:
                    exps(s, t + 1, 1 - b)
                if s == 0:
                    act.wait_ge(s_pt, t + 1)
                    act.activation(ptt[:, :, :], pS[:, 0:KD * P], ACT.Copy).then_inc(s_ptc, 1)
                for q in range(NCH):
                    act.wait_ge(s_emu, NCH * (s * NT + t) + q + 1)
                    if q == 0:
                        if some(s * NT + t):
                            act.wait_ge(s_A, s * NT + t)
                    act.activation(emt[:, 4 * q:4 * q + 4, :], pT[q % 2][:, :], ACT.Copy).then_inc(s_et, 1)
                if s == 0:
                    act.wait_ge(s_A, t + 1)
                    act.wait_ge(s_dinv, t + 1)
                    act.activation(xst[:, :], pA[:, 0:D], ACT.Copy, scale=dinv[:, b:b + 1]).then_inc(s_Ae, 1)
                    act.wait_ge(s_at, t + 1)
                    act.activation(xtt[:, :, :], pA[:, 0:KD * P], ACT.Copy).then_inc(s_atc, 1)
                    act.activation(xt[:, :, rows(t)], pA[:, 0:KD * P].rearrange("p (k i) -> p k i", k=KD), ACT.Copy).then_inc(s_atc, 1)

            for s in range(2):
                if s == 0:
                    xt_copies(s)
                qk_high(s)
                exps(s, 0, 0)
                if s == 0:
                    tile(s, 0, 0, True)
                    tile(s, 1, 1, True)
                    with act.Fori(1, NP - 1) as q:
                        for b in range(2):
                            tile(s, 2 * q + b, b, True)
                else:
                    with act.Fori(0, NP - 1) as q:
                        for b in range(2):
                            tile(s, 2 * q + b, b, True)
                tile(s, NT - 2, 0, True)
                tile(s, NT - 1, 1, False)

            act.wait_ge(s_nrm, 2)
            for t in range(NT):
                act.activation(r3[:, t, :], pu2[:, t, :], ACT.Relu, bias=nmr[:, t:t + 1],
                               scale=rstd[:, t:t + 1]).then_inc(s_h1, 1)
            xt_copies(1)
            act.wait_ge(s_slb, NT)
            act.activation(slb[:, :], pL[:, :], ACT.Copy).then_inc(s_slc, 1)
            def l1_tile(t):
                act.wait_ge(s_lr, t + 1)
                act.activation(lrb, lrb, ACT.Exp, scale=-1.0).then_inc(s_ex, 1)
                act.wait_ge(s_gz, t + 1)
                act.activation(ge[:, :], gz[:, :], ACT.Exp, scale=-1.0).then_inc(s_ge, 1)
                act.wait_ge(s_y, t + 1)
                act.activation(fe[:, 0, :], fe[:, 1, :], ACT.Exp, scale=-1.0).then_inc(s_ye, 1)
                act.wait_ge(s_fin, t + 1)
                act.dma_start(out_d[bass.ds(t * P, P), :], fin[:, 0, :]).then_inc(s_out, 16)
                act.wait_ge(s_out, 16 * t + 16)

            l1_tile(0)
            with act.Fori(1, NT) as t:
                l1_tile(t)
            act.wait_ge(s_out, 16 * NT)

        @block.vector
        def _(dve):
            link_base = [0]
            link_n = [0]

            def link(ins):
                link_n[0] += 1
                ins.then_inc(s_dve, 1)
                dve.wait_ge(s_dve, link_base[0] + link_n[0])

            def loop(lo_, hi_, body, links):
                start = link_base[0] + link_n[0]
                with dve.Fori(lo_, hi_) as q:
                    link_base[0] = start + (q - lo_) * links
                    link_n[0] = 0
                    body(q)
                    assert link_n[0] == links, (link_n[0], links)
                link_base[0] = start + (hi_ - lo_) * links
                link_n[0] = 0

            def norm(n, src):
                for t in range(NT):
                    ins = dve.bn_stats(stats[:, t, :], src[:, t, 0:D])
                link(ins)
                for t in range(NT):
                    ins = dve.bn_aggr(mv[:, t, :], stats[:, t, :])
                link(ins)
                dve.tensor_scalar(tn[:, :], mv[:, :, 1], LN_EPS, None, ALU.add).then_inc(s_var, 1)
                dve.wait_ge(s_pow, n + 1)
                link(dve.tensor_tensor(nmr[:, :], rstd[:, :], rstd[:, :], ALU.mult))
                link(dve.tensor_tensor(nmr[:, :], nmr[:, :], tn[:, :], ALU.mult))
                link(dve.tensor_scalar(nmr[:, :], nmr[:, :], -0.5, 1.5, ALU.mult, ALU.add))
                link(dve.tensor_tensor(rstd[:, :], rstd[:, :], nmr[:, :], ALU.mult))
                link(dve.scalar_tensor_tensor(nmr[:, :], mv[:, :, 0], -1.0, rstd[:, :], ALU.mult, ALU.mult))

            dve.memset(xc[:, :, D:D + 1], 1.0).then_inc(s_col, 1)
            dve.wait_ge(s_x, 16)
            norm(0, r3)
            dve.nop().then_inc(s_nrm, 1)

            def qk_low(s):
                for n in range(NCH):
                    cols = slice(n * CH, (n + 1) * CH)
                    dve.wait_ge(s_qh[0], NCH * s + n + 1)
                    dve.scalar_tensor_tensor(qs[DA:P, cols], pT[0][DA:P, :], SQK, qs[DA:P, cols],
                                             ALU.mult, ALU.subtract).then_inc(s_qe[0], 1)
                    dve.wait_ge(s_qh[1], NCH * s + n + 1)
                    dve.scalar_tensor_tensor(kl[:, cols], pT[1][:, :], SQK, kh[:, cols],
                                             ALU.mult, ALU.subtract).then_inc(s_qe[1], 1)

            def row_max(s, t, b):
                dve.wait_ge(s_L, s * NT + t + 1)
                link(dve.tensor_reduce(nmax[:, b:b + 1], pL[:, :], AX.X, ALU.max))
                dve.tensor_scalar(nbias[:, b:b + 1], nmax[:, b:b + 1], -LSCALE, None, ALU.mult).then_inc(s_max, 1)

            def threshold(s, t, b):
                dve.wait_ge(s_e, s * NT + t + 1)
                if some(NCH * (s * NT + t)):
                    dve.wait_ge(s_emu, NCH * (s * NT + t))
                dve.tensor_scalar(target[:, :], zsum[:, b:b + 1], P_NUC, None, ALU.mult)
                dve.tensor_scalar(probe[:, :], zsum[:, b:b + 1], FLOOR * math.exp(WIDTH / 2), None, ALU.mult)
                link(dve.tensor_scalar(lo[:, :], zsum[:, b:b + 1], FLOOR, None, ALU.mult))
                for n in range(PASSES):
                    link(dve.scalar_tensor_tensor(junk[:, :], ew[:, b, :], probe[:, :], ew[:, b, :],
                                                  ALU.is_ge, ALU.mult, accum_out=mass[:, :]))
                    link(dve.scalar_tensor_tensor(hit[:, :], mass[:, :], target[:, :], probe[:, :], ALU.is_ge, ALU.mult))
                    dve.tensor_scalar(probe[:, :], hit[:, :], lo[:, :], math.exp(WIDTH / 2 ** (n + 2)), ALU.max, ALU.mult)
                    link(dve.tensor_tensor(lo[:, :], hit[:, :], lo[:, :], ALU.max))

            def tile(s, t, b, more):
                if more:
                    row_max(s, t + 1, 1 - b)
                if s == 0:
                    dve.wait_ge(s_S, t + 1)
                    if some(t):
                        dve.wait_ge(s_pt, t)
                    dve.tensor_tensor(pst[:, :], pS[:, 0:D + 1], xc[:, bass.ds(t, 1), 0:D + 1].rearrange("p a n -> p (a n)"),
                                      ALU.add).then_inc(s_Se, 1)
                    dve.wait_ge(s_Se, t + 1)
                    link(dve.tensor_scalar(den[:, :], pst[:, D:D + 1], 1e-12, None, ALU.max))
                    link(dve.reciprocal(rinv[:, bass.ds(t, 1)], den[:, :]))
                else:
                    dve.wait_ge(s_S, NT + t + 1)
                    gt = g[:, bass.ds(t, 1), :].rearrange("p a n -> p (a n)")
                    zt = z[:, bass.ds(t, 1), :].rearrange("p a n -> p (a n)")
                    pt = pu2[:, bass.ds(t, 1), :].rearrange("p a n -> p (a n)")
                    ins = dve.tensor_tensor(w[:, :], pS[:, :], gt, ALU.add)
                    ins.then_inc(s_Se, 1)
                    dve.wait_ge(s_Se, NT + t + 1)
                    link(dve.scalar_tensor_tensor(zt, w[:, 0:D], rinv[:, bass.ds(t, 1)], zt, ALU.mult, ALU.add))
                    link(dve.tensor_tensor(w[:, 0:D], w[:, D:2 * D], pt, ALU.add))
                    link(dve.scalar_tensor_tensor(zt, w[:, 0:D], cinv[:, bass.ds(t, 1)], zt, ALU.mult, ALU.add))
                threshold(s, t, b)
                dve.scalar_tensor_tensor(em[:, :], ew[:, b, :], lo[:, :], ew[:, b, :], ALU.is_ge, ALU.mult,
                                         accum_out=den[:, :]).then_inc(s_em, 1)
                dve.wait_ge(s_em, s * NT + t + 1)
                dve.reciprocal(dinv[:, b:b + 1], den[:, :]).then_inc(s_dinv, 1)
                if s == 0:
                    dve.wait_ge(s_PU, t + 1)
                    xrow = xc[:, bass.ds(t, 1), 0:D].rearrange("p a n -> p (a n)")
                    zt = z[:, bass.ds(t, 1), :].rearrange("p a n -> p (a n)")
                    rt = rinv[:, bass.ds(t, 1)]
                    dve.scalar_tensor_tensor(zt, pT[0][:, 0:D], rt, xrow, ALU.mult, ALU.add)
                    dve.tensor_copy(pu2[:, bass.ds(t, 1), :].rearrange("p a n -> p (a n)"), pT[0][:, D:2 * D])
                    dve.tensor_scalar(g[:, bass.ds(t, 1), 0:D].rearrange("p a n -> p (a n)"), pT[1][:, 0:D], rt, None, ALU.mult)
                    dve.tensor_copy(g[:, bass.ds(t, 1), D:2 * D].rearrange("p a n -> p (a n)"), pT[1][:, D:2 * D]).then_inc(s_PUe, 1)
                    dve.wait_ge(s_PUe, t + 1)
                    dve.wait_ge(s_AU, t + 1)
                    dve.tensor_tensor(zt, pT[0][:, 0:D], zt, ALU.add)
                    dve.tensor_copy(r3[:, bass.ds(t, 1), :].rearrange("p a n -> p (a n)"), pT[0][:, D:2 * D]).then_inc(s_AUe, 1)
                    dve.wait_ge(s_AUe, t + 1)
                else:
                    dve.wait_ge(s_A, NT + t + 1)
                    dve.wait_ge(s_dinv, NT + t + 1)
                    zt = z[:, bass.ds(t, 1), :].rearrange("p a n -> p (a n)")
                    dve.scalar_tensor_tensor(zt, pA[:, 0:D], dinv[:, b:b + 1], zt, ALU.mult, ALU.add).then_inc(s_Ae, 1)
                    dve.wait_ge(s_Ae, NT + t + 1)

            per_tile = {0: 1 + 2 + 1 + 3 * PASSES, 1: 1 + 3 + 1 + 3 * PASSES}
            for s in range(2):
                qk_low(s)
                row_max(s, 0, 0)

                def pair(q):
                    for b in range(2):
                        tile(s, 2 * q + b, b, True)

                if s == 0:
                    pair(0)
                loop(1 - s, NP - 1, pair, 2 * per_tile[s])
                tile(s, NT - 2, 0, True)
                tile(s, NT - 1, 1, False)
                if s == 0:
                    dve.wait_ge(s_pool, 2 * NT + 1)
                    link(dve.tensor_reduce(cinv[:, :], cacc[:, :, :], AX.X, ALU.add))
                    link(dve.tensor_scalar(cinv[:, :], cinv[:, :], 1.0, 1e-12, ALU.add, ALU.max))
                    link(dve.reciprocal(cinv[:, :], cinv[:, :]))
                    dve.tensor_tensor(g[:, :, D:2 * D], g[:, :, D:2 * D],
                                      cinv[:, :].rearrange("p (t a) -> p t a", a=1).to_broadcast([P, NT, D]),
                                      ALU.mult).then_inc(s_gs, 1)

            norm(1, z)
            dve.wait_ge(s_x2, 16)
            for t in range(NT):
                ins = dve.tensor_scalar(z[:, t, :], z[:, t, :], rstd[:, t:t + 1], nmr[:, t:t + 1], ALU.mult, ALU.add)
            link(ins)
            link(dve.tensor_tensor(z[:, :, :], z[:, :, :], gamma[:, :].rearrange("p (a n) -> p a n", a=1).to_broadcast([P, NT, D]), ALU.mult))
            link(dve.tensor_tensor(z[:, :, :], z[:, :, :], beta[:, :].rearrange("p (a n) -> p a n", a=1).to_broadcast([P, NT, D]), ALU.add))
            link(dve.tensor_tensor(pu2[:, :, :], z[:, :, :], xc[:, :, 0:D], ALU.add))
            norm(2, pu2)
            dve.nop().then_inc(s_nrm, 1)
            dve.memset(h257[:, :, D:D + 1], 1.0).then_inc(s_col, 1)

            for t in range(NT):
                dve.wait_ge(s_m, t + 1)
                dve.tensor_copy(h257[:, t, 0:D], pT[0][:, 0:D])
                dve.tensor_copy(xgate[:, t, D:D + 2], pT[0][:, D:D + 2])
                dve.tensor_copy(ga[:, t, :], pT[0][:, D + 2:D + 4])
                link(dve.tensor_copy(xgate[:, t, 0:D], pT[1][:, 0:D]))
                dve.scalar_tensor_tensor(w[:, 0:D], h257[:, t, 0:D], 1.0, asa[:, 0:D], ALU.mult, ALU.mult,
                                         accum_out=sl[:, t:t + 1])
                link(dve.scalar_tensor_tensor(w[:, D:2 * D], h257[:, t, 0:D], 1.0, asa[:, D:2 * D], ALU.mult, ALU.mult,
                                              accum_out=sr[:, t:t + 1]))
                dve.nop().then_inc(s_me, 1)
            for t in range(NT):
                if t >= 2:
                    dve.wait_ge(s_slb, t - 1)
                dve.tensor_scalar(emt[:, t % 2, :], ident[:, :], sl[:, t:t + 1], None, ALU.mult).then_inc(s_diag, 1)

            def l1_tile(t, q, b):
                dve.wait_ge(s_sco, t + 1)
                if some(t):
                    dve.wait_ge(s_mk, t)
                dve.scalar_tensor_tensor(lrb, sco, 0.01, sco, ALU.mult, ALU.max).then_inc(s_lr, 1)
                dve.wait_ge(s_ex, t + 1)
                dve.wait_ge(s_adj[b], 16 * (2 * NP + q) + 16)
                if some(t):
                    dve.wait_ge(s_xa, t)
                dve.scalar_tensor_tensor(edge[:, :], adjb[:, b, :], 0.0, lrb, ALU.not_equal, ALU.mult).then_inc(s_mk, 1)
                dve.wait_ge(s_xb, t + 1)
                if some(t):
                    dve.wait_ge(s_ge, t)
                gat = ga[:, bass.ds(t, 1), :].rearrange("p a n -> p (a n)")
                link(dve.tensor_tensor(gz[:, :], pS[:, D:D + 2], gat, ALU.add))
                dve.tensor_tensor(gz[:, :], gz[:, :], bab[:, :], ALU.add).then_inc(s_gz, 1)
                link(dve.tensor_tensor(fe[:, 1, :], pS[:, 0:D], bg[:, :], ALU.add))
                dve.wait_ge(s_ge, t + 1)
                link(dve.tensor_scalar(ge[:, :], ge[:, :], 1.0, None, ALU.add))
                link(dve.reciprocal(ge[:, :], ge[:, :]))
                dve.wait_ge(s_xa, t + 1)
                link(dve.tensor_scalar(den[:, :], pA[:, D:D + 1], 1e-5, None, ALU.add))
                link(dve.reciprocal(den[:, :], den[:, :]))
                link(dve.tensor_tensor(den[:, :], den[:, :], ge[:, 0:1], ALU.mult))
                link(dve.tensor_scalar(fe[:, 1, :], fe[:, 1, :], ge[:, 1:2], None, ALU.mult))
                dve.scalar_tensor_tensor(fe[:, 1, :], pA[:, 0:D], den[:, :], fe[:, 1, :], ALU.mult, ALU.add).then_inc(s_y, 1)
                dve.wait_ge(s_y, t + 1)
                dve.nop().then_inc(s_rd, 1)
                dve.wait_ge(s_ye, t + 1)
                link(dve.tensor_scalar(fe[:, 0, :], fe[:, 0, :], 1.0, None, ALU.add))
                link(dve.reciprocal(fe[:, 0, :], fe[:, 0, :]))
                if some(16 * t):
                    dve.wait_ge(s_out, 16 * t)
                dve.tensor_tensor(fin[:, 0, :], fe[:, 0, :], pu2[:, bass.ds(t, 1), :].rearrange("p a n -> p (a n)"), ALU.add).then_inc(s_fin, 1)

            def l1_pair(q):
                for b in range(2):
                    l1_tile(2 * q + b, q, b)

            l1_pair(0)
            loop(1, NP, l1_pair, 2 * 10)

        @block.tensor
        def _(pe):
            def mm(out, lhs, rhs, k, n):
                return pe.matmul(out, lhs, rhs, start=(k == 0), stop=(k == n - 1))

            pe.wait_ge(s_wts, WTS)
            for k in range(KD):
                ins = mm(pS[:, k * P:(k + 1) * P], w1t[:, k * P:(k + 1) * P], w22[:, :], 0, 1)
            ins.then_inc(s_w12p, 1)

            def x_transposes(s, src, ready):
                for n in range(KD * NCH):
                    k, c, b = n % KD, n // KD, n % 2
                    pe.wait_ge(ready, 4 * c + 4)
                    if n >= 2 or s > 0:
                        pe.wait_ge(s_te[b], 4 * s + n // 2)
                    for m in range(4):
                        ins = pe.transpose(pT[b][:, m * P:(m + 1) * P], src[:, 4 * c + m, k * P:(k + 1) * P], ident[:, :])
                    ins.then_inc(s_tp[b], 1)

            def qk(s):
                for n in range(NCH):
                    for b, wt in ((0, w12), (1, w33)):
                        if n > 0 or s > 0:
                            pe.wait_ge(s_qe[b], NCH * s + n)
                        if n == 0 and s == 0:
                            pe.wait_ge(s_te[b], 4)
                        if n == 0 and s > 0:
                            pe.wait_ge(s_AUe, NT)
                        for k in range(KD):
                            ins = mm(pT[b][:, :], wt[:, k, :], xt[:, k, n * CH:(n + 1) * CH], k, KD)
                        ins.then_inc(s_qp[b], 1)

            def logits(s, t):
                if s > 0 or not isinstance(t, int) or t > 0:
                    pe.wait_ge(s_e, s * NT + t)
                for n in range(NCH):
                    cols = slice(n * CH, (n + 1) * CH)
                    mm(pL[:, cols], qs[:, bass.ds(t * P, P)], kh[:, cols], 0, 2)
                    ins = mm(pL[:, cols], qs[:, bass.ds(t * P, P)], kl[:, cols], 1, 2)
                ins.then_inc(s_L, 1)

            def tile(s, t, q, b, more):
                if more:
                    logits(s, t + 1)
                pe.wait_ge(s_adj[b], 16 * (s * NP + q) + 16)
                rhs = xc if s == 0 else g
                width = D + 1 if s == 0 else 2 * D
                if s == 0:
                    if some(t):
                        pe.wait_ge(s_ptc, t)
                else:
                    pe.wait_ge(s_Se, NT + t)
                for j in range(NT):
                    ins = mm(pS[:, 0:width], adjb[:, b, j * P:(j + 1) * P], rhs[:, j, 0:width], j, NT)
                ins.then_inc(s_S, 1)
                pe.wait_ge(s_S, s * NT + t + 1)
                pe.nop().then_inc(s_adjf[b], 1)
                if s == 0:
                    pe.wait_ge(s_Se, t + 1)
                    for k in range(KD):
                        ins = pe.transpose(pS[:, k * P:(k + 1) * P], pst[:, k * P:(k + 1) * P], ident[:, :])
                    ins.then_inc(s_pt, 1)
                pe.wait_ge(s_em, s * NT + t + 1)
                if s == 0:
                    if some(t):
                        pe.wait_ge(s_AUe, t)
                for c in range(NCH):
                    if c >= 2:
                        pe.wait_ge(s_et, NCH * (s * NT + t) + c - 1)
                    elif s > 0:
                        pe.wait_ge(s_et, NCH * (s * NT + t))
                    for m in range(4):
                        col = (4 * c + m) * P
                        ins = pe.transpose(pT[c % 2][:, m * P:(m + 1) * P], em[:, col:col + P], ident[:, :])
                    ins.then_inc(s_emu, 1)
                if s == 1:
                    pe.wait_ge(s_Ae, NT + t)
                    rhs = r3
                for j in range(NT):
                    if j % 4 == 0:
                        pe.wait_ge(s_et, NCH * (s * NT + t) + j // 4 + 1)
                    ins = mm(pA[:, 0:D], emt[:, j, :], (xc if s == 0 else r3)[:, j, 0:D], j, NT)
                ins.then_inc(s_A, 1)
                if s == 0:
                    pe.wait_ge(s_ptc, t + 1)
                    for k in range(KD):
                        mm(pT[0][:, :], ptt[:, k, :], u12a[:, k, :], k, KD)
                    for k in range(KD):
                        ins = mm(pT[1][:, :], ptt[:, k, :], u12b[:, k, :], k, KD)
                    ins.then_inc(s_PU, 1)
                    pe.wait_ge(s_Ae, t + 1)
                    for k in range(KD):
                        ins = pe.transpose(pA[:, k * P:(k + 1) * P], xst[:, k * P:(k + 1) * P], ident[:, :])
                    ins.then_inc(s_at, 1)
                    pe.wait_ge(s_PUe, t + 1)
                    pe.wait_ge(s_atc, 2 * t + 1)
                    for k in range(KD):
                        ins = mm(pT[0][:, :], xtt[:, k, :], u3[:, k, :], k, KD)
                    ins.then_inc(s_AU, 1)
                    pe.wait_ge(s_atc, 2 * t + 2)

            for s in range(2):
                if s == 0:
                    pe.wait_ge(s_col, 1)
                    x_transposes(0, xc, s_xc)
                    for b in range(2):
                        pe.wait_ge(s_te[b], 4)
                    pe.wait_ge(s_w12, 1)
                qk(s)
                for b in range(2):
                    pe.wait_ge(s_qe[b], NCH * (s + 1))
                if s == 1:
                    pe.wait_ge(s_gs, 1)
                logits(s, 0)
                if s == 0:
                    tile(s, 0, 0, 0, True)
                    tile(s, 1, 0, 1, True)
                with pe.Fori(1 - s, NP - 1) as q:
                    for b in range(2):
                        tile(s, 2 * q + b, q, b, True)
                tile(s, NT - 2, NP - 1, 0, True)
                tile(s, NT - 1, NP - 1, 1, False)

            x_transposes(1, r3, s_h1)
            for b in range(2):
                pe.wait_ge(s_te[b], 8)
            for t in range(NT):
                if t >= 1:
                    pe.wait_ge(s_me, t)
                for k in range(KD):
                    mm(pT[0][:, 0:D + 4], xt[:, k, t * P:(t + 1) * P], wsg[:, k, :], k, KD)
                for k in range(KD):
                    ins = mm(pT[1][:, 0:D], xt[:, k, t * P:(t + 1) * P], wg[:, k, :], k, KD)
                ins.then_inc(s_m, 1)
            pe.wait_ge(s_me, NT)
            pe.wait_ge(s_col, 2)
            pe.wait_ge(s_ms, 2)
            for t in range(NT):
                pe.wait_ge(s_diag, t + 1)
                mm(pL[:, t * P:(t + 1) * P], ones[:, :], emt[:, t % 2, :], 0, 1).then_inc(s_slb, 1)

            def l1_pair(q):
                for b in range(2):
                    t = 2 * q + b
                    pe.wait_ge(s_adj[b], 16 * (2 * NP + q) + 16)
                    if some(t):
                        pe.wait_ge(s_rd, t)
                    for j in range(NT):
                        ins = mm(pS[:, 0:D + 2], adjb[:, b, j * P:(j + 1) * P], xgate[:, j, :], j, NT)
                    ins.then_inc(s_xb, 1)
                    pe.wait_ge(s_mk, t + 1)
                    for j in range(NT):
                        ins = mm(pA[:, 0:D + 1], edge[:, j * P:(j + 1) * P], h257[:, j, :], j, NT)
                    ins.then_inc(s_xa, 1)
                    pe.wait_ge(s_xb, t + 1)
                    pe.nop().then_inc(s_adjf[b], 1)

            l1_pair(0)
            with pe.Fori(1, NP) as q:
                l1_pair(q)

    return nc


_IDENT = np.eye(128, dtype=np.float32)


def kernel(x, adj, L0_gnn_W1, L0_gnn_W2, L0_gnn_W3, L0_gnn_U1, L0_gnn_U2, L0_gnn_U3, L0_gnn_gamma, L0_gnn_beta,
           L1_gnn_W_sa, L1_gnn_a_sa, L1_gnn_W_gcnb, L1_gnn_b_gcnb, L1_gnn_Wa, L1_gnn_ba, L1_gnn_Wb, L1_gnn_bb):
    import concourse.bacc as bacc
    from concourse.bass_utils import run_bass_kernel_spmd

    x = np.asarray(x)
    adj = np.asarray(adj)
    n, d = x.shape
    nt = n // 128
    wa, wb = np.asarray(L1_gnn_Wa), np.asarray(L1_gnn_Wb)
    arrays = {
        "x": x,
        "adjt": np.asarray(adj).reshape(nt, 128, nt, 128).transpose(0, 3, 2, 1).reshape(nt, 128, n),
        "w1t": np.asarray(L0_gnn_W1).T,
        "w2": L0_gnn_W2, "w3": L0_gnn_W3, "u1": L0_gnn_U1, "u2": L0_gnn_U2, "u3": L0_gnn_U3,
        "gamma": L0_gnn_gamma, "beta": L0_gnn_beta,
        "wsa": L1_gnn_W_sa, "asa": np.asarray(L1_gnn_a_sa).reshape(2 * d), "wg": L1_gnn_W_gcnb, "bg": L1_gnn_b_gcnb,
        "wgate": np.stack([wa[0, :d], wb[0, :d], wa[0, d:], wb[0, d:]], axis=1),
        "ba": L1_gnn_ba, "bb": L1_gnn_bb, "ident": _IDENT,
    }
    arrays = {k: np.ascontiguousarray(np.asarray(v)) for k, v in arrays.items()}
    nc = bacc.Bacc("TRN2", target_bir_lowering=False, num_devices=1)
    args = [nc.dram_tensor(f"in_{k}", v.shape, mybir.dt.from_np(v.dtype), kind="ExternalInput").ap() for k, v in arrays.items()]
    out = nc.dram_tensor("out_x", (n, d), mybir.dt.float32, kind="ExternalOutput").ap()
    gnn_block_program(nc, *args, out)
    r = run_bass_kernel_spmd(nc, [{f"in_{k}": v for k, v in arrays.items()}], core_ids=[0])
    return r.results[0]["out_x"]
```

```python
import math

import numpy as np

import concourse.bass as bass
from concourse import mybir
from contextlib import ExitStack


def gnn_block_program(nc, x_d, adjt_d, w1t_d, w2_d, w3_d, u1_d, u2_d, u3_d, gamma_d, beta_d,
                      wsa_d, asa_d, wg_d, bg_d, wgate_d, ba_d, bb_d, ident_d, pu2_d, zs_d, out_d):
    F32 = mybir.dt.float32
    F16 = mybir.dt.float16
    I32 = mybir.dt.int32
    ALU = mybir.AluOpType
    ACT = mybir.ActivationFunctionType
    AX = mybir.AxisListType
    ADD = bass.bass_isa.ReduceOp.add

    P = 128
    N, D = x_d.shape
    NT = N // P
    KD = D // P
    DA = w2_d.shape[0]
    NP = NT // 2
    G4 = 4
    NQ = NT // G4
    CH = 512
    NCH = N // CH
    LN_EPS = 1e-5
    P_NUC = 0.9
    SQK = 64.0
    LSCALE = 1.0 / (SQK * SQK)

    FLOOR = (1.0 - P_NUC) / N
    TOP = 1.0001
    BIG = 1.0e30
    PROBES = ("ggggi", "gggiiiiii")
    AIM = (5.0, 6.0)
    CLIP = 0.9
    NEAR = 7.0
    GEO = 4
    HALVINGS = 3 * 14

    ctx = ExitStack()
    with ctx:
        def sb(name, shape, dt=F32):
            return ctx.enter_context(nc.sbuf_tensor(name, shape, dt))

        def ps(name, shape):
            return ctx.enter_context(nc.psum_tensor(name, shape, F32))

        def some(count):
            return not isinstance(count, int) or count > 0

        def sem(name):
            return ctx.enter_context(nc.semaphore(name))

        ident = sb("ident", [P, P])
        ones = sb("ones", [P, P])
        w1t = sb("w1t", [DA, D])
        w22 = sb("w22", [DA, 2 * DA])
        w33 = sb("w33", [P, KD, 2 * DA])
        w12 = sb("w12", [P, KD, 2 * DA])
        u12 = sb("u12", [P, 8 * D])
        u12a = u12[:, 0:4 * D].rearrange("p (k n) -> p k n", k=KD)
        u12b = u12[:, 4 * D:8 * D].rearrange("p (k n) -> p k n", k=KD)
        u3 = sb("u3", [P, KD, 2 * D])
        gamma = sb("gamma", [P, D])
        beta = sb("beta", [P, D])
        WS = KD * (D + 4)
        wsg = u12[:, 0:WS].rearrange("p (k n) -> p k n", k=KD)
        wg = u12[:, WS:WS + KD * D].rearrange("p (k n) -> p k n", k=KD)
        asa = u12[:, WS + KD * D:WS + KD * D + 2 * D]
        bg = u12[:, WS + KD * D + 2 * D:WS + KD * D + 3 * D]
        bab = sb("bab", [P, 2])

        xc = sb("xc", [P, NT, D + 2])
        xt = sb("xt", [P, KD, N])
        qs = sb("qs", [P, N], F16)
        kh = sb("kh", [P, N], F16)
        kl = sb("kl", [P, N], F16)
        ew = sb("ew", [P, G4, N])
        em = sb("em", [P, 2, N])
        emt = sb("emt", [P, NT, P])
        junk = sb("junk", [P, 2, N], mybir.dt.uint8)
        adjb = sb("adjb", [P, 2, N])
        cacc = sb("cacc", [P, NT, P // 2])
        pst = sb("pst", [P, D + 1])
        pair_t = sb("pair_t", [P, 2, KD, P])
        ptt = pair_t[:, 0, :, :]
        xst = sb("xst", [P, D])
        xtt = pair_t[:, 1, :, :]
        w = pair_t[:, :, :, :].rearrange("p a k n -> p (a k n)")
        tz = sb("tz", [P, 2, D])
        ta = sb("ta", [P, D])
        z = xc[:, :, 0:D]
        zq = sb("zq", [P, G4, D])
        pu2 = sb("pu2", [P, 2, D])
        g = sb("g", [P, NT, 2 * D])
        r3 = sb("r3", [P, NT, D + 2])
        stats = sb("stats", [P, NT, 6])
        mv = sb("mv", [P, NT, 2])
        rstd = sb("rstd", [P, NT])
        nmr = sb("nmr", [P, NT])
        tn = sb("tn", [P, NT])
        half = sb("half", [P, NT])
        rinv = sb("rinv", [P, NT])
        cinv = sb("cinv", [P, NT])
        sl = sb("sl", [P, NT])
        sr = sb("sr", [P, NT])
        ga = sb("ga", [P, NT, 2])
        gz = sb("gz", [P, 2])
        ge = sb("ge", [P, 2])
        den = sb("den", [P, 1])

        nmax = sb("nmax", [P, G4])
        nbias = sb("nbias", [P, G4])
        zsum = sb("zsum", [P, G4])
        target = sb("target", [P, G4])
        low0 = sb("low0", [P, G4])
        cur = sb("cur", [P, G4, 2])
        lo = sb("lo", [P, G4, 2])
        hi = sb("hi", [P, G4, 2])
        gap = sb("gap", [P, G4, 2])
        mass = sb("mass", [P, G4])
        is_lo = sb("is_lo", [P, G4], I32)
        is_hi = sb("is_hi", [P, G4], I32)
        qa = sb("qa", [P, G4])
        qb = sb("qb", [P, G4])
        expo = sb("expo", [P, G4, GEO])
        step = sb("step", [P, G4, GEO])
        top8 = sb("top8", [P, G4, 8])
        pre8 = sb("pre8", [P, G4, 8])
        abv8 = sb("abv8", [P, G4, 8])
        cut8 = sb("cut8", [P, G4, 8], I32)
        big8 = sb("big8", [P, G4, 8])
        zero8 = sb("zero8", [P, 8])
        tf = sb("tf", [P, G4])
        above = sb("above", [P, G4])
        short = sb("short", [P, G4])
        ties = sb("ties", [P, G4])
        kept = sb("kept", [P, G4])
        flags = sb("flags", [P, 2])
        flagi = sb("flagi", [P, 2], I32)
        again = sb("again", [P, 32])
        againt = sb("againt", [P, 32])
        anyr = sb("anyr", [P, 1], I32)
        dinv = sb("dinv", [P, G4])

        pL = ps("pL", [P, N])
        pT = [ps("pT0", [P, CH]), ps("pT1", [P, CH])]
        pS = ps("pS", [P, CH])
        pA = ps("pA", [P, CH])

        s_wts = sem("weights_loaded")
        s_l1w = sem("l1_weights_loaded")
        s_x = sem("x_loaded")
        s_x2 = sem("x_loaded_again")
        s_adj = [sem("adj_loaded0"), sem("adj_loaded1")]
        s_adjf = [sem("adj_used0"), sem("adj_used1")]
        s_csum = [sem("adj_summed0"), sem("adj_summed1")]
        s_pust = [sem("pu2_stored0"), sem("pu2_stored1")]
        s_puld = [sem("pu2_loaded0"), sem("pu2_loaded1")]
        s_pgo = sem("pool_past_waits")
        s_vgo = sem("vector_past_waits")
        s_zst = [sem(f"z_stored{b}") for b in range(G4)]
        s_zld = sem("z_loaded")
        s_out = [sem("out_stored0"), sem("out_stored1")]
        s_dve = sem("dve_chain")
        s_fb = sem("branch_chain")
        s_pool = sem("pool_chain")
        s_ms = sem("constants_set")
        s_dms = sem("search_constants_set")
        s_col = sem("column_of_ones")
        s_var = sem("variance_ready")
        s_pow = sem("rsqrt_guess_ready")
        s_low = sem("floor_ready")
        s_step = sem("steps_ready")
        s_nrm = sem("norm_ready")
        s_xc = sem("x_normed")
        s_w12p = sem("w12_product")
        s_w12 = sem("w12_ready")
        s_tp = [sem("transposed0"), sem("transposed1")]
        s_te = [sem("transpose_copied0"), sem("transpose_copied1")]
        s_qp = [sem("qk_product0"), sem("qk_product1")]
        s_qe = [sem("qk_split0"), sem("qk_split1")]
        s_qh = [sem("qk_high0"), sem("qk_high1")]
        s_L = sem("logits_ready")
        s_max = sem("max_ready")
        s_e = sem("exp_ready")
        s_fl = sem("flags_ready")
        s_fa = sem("flags_summed")
        s_em = sem("kept_ready")
        s_dinv = sem("kept_mass_inverted")
        s_emu = sem("kept_transposed")
        s_et = sem("kept_columns_copied")
        s_A = sem("attention_product")
        s_Ae = sem("attention_copied")
        s_S = sem("adjacency_product")
        s_Se = sem("adjacency_copied")
        s_rinv = sem("row_sum_inverted")
        s_pt = sem("p_transposed")
        s_ptc = sem("p_columns_copied")
        s_PU = sem("p_u_products")
        s_pu0 = sem("pu1_scaled")
        s_puc = sem("pu2_copied")
        s_PUe = sem("p_u_products_read")
        s_zs = sem("z_added_s")
        s_za = sem("z_added_a")
        s_at = sem("ax_transposed")
        s_atc = sem("ax_columns_copied")
        s_AU = sem("ax_u3_product")
        s_AUa = sem("ax_u3_copied")
        s_AUe = sem("ax_u3_product_read")
        s_gs = sem("g_scaled")
        s_h1 = sem("h1_ready")
        s_m = sem("h_products")
        s_me = sem("h_products_read")
        s_diag = sem("diag_ready")
        s_slb = sem("s_left_spread")
        s_slc = sem("s_left_copied")
        s_sco = sem("scores_ready")
        s_lr = sem("leaky_ready")
        s_ex = sem("edge_exp_ready")
        s_mk = sem("edge_weights_ready")
        s_xa = sem("xa_product")
        s_xb = sem("xb_product")
        s_rd = sem("products_read")
        s_gz = sem("gate_logits")
        s_ge = sem("gate_exp")
        s_y = sem("y_ready")
        s_ye = sem("y_exp")
        s_fin = sem("out_tile_ready")

        sco, edge = ew, em
        fe = ew[:, 2, 0:2 * D].rearrange("p (a n) -> p a n", a=2)
        fin = ew[:, 3, 0:2 * D].rearrange("p (a n) -> p a n", a=2)
        slb = g[:, :, :].rearrange("p t n -> p (t n)")[:, NT * 2 * D - N:]
        h257 = g[:, :, :].rearrange("p t n -> p (t n)")[:, 0:NT * (D + 1)].rearrange("p (t n) -> p t n", t=NT)
        x_again = g[:, :, :].rearrange("p t n -> p (t n)")[:, 0:NT * D].rearrange("p (t n) -> p t n", t=NT)
        xgate = r3
        WTS = 16 * 14
        WL1 = 16 * 7

        def tile_of(buf, t, c0, c1):
            return buf[:, bass.ds(t, 1), c0:c1].rearrange("p a n -> p (a n)")

        def quads(eng, s, body):
            if s == 0:
                body(0, True)
            with eng.Fori(1 - s, NQ - 1) as q:
                body(q, True)
            body(NQ - 1, False)

        block = ctx.enter_context(nc.Block())

        @block.sync
        def _(sp):
            sp.dma_start(r3[:, :, 0:D], x_d.rearrange("(t p) n -> p t n", p=P)).then_inc(s_x, 16)
            loads = [(ident[:, :], ident_d), (w1t[:, :], w1t_d),
                     (w22[:, 0:DA], w2_d), (w22[:, DA:2 * DA], w2_d),
                     (w33[:, :, 0:DA], w3_d.rearrange("(k p) n -> p k n", p=P)),
                     (w33[:, :, DA:2 * DA], w3_d.rearrange("(k p) n -> p k n", p=P)),
                     (gamma[:, :], gamma_d.partition_broadcast(P)), (beta[:, :], beta_d.partition_broadcast(P))]
            for s in range(2):
                for dst, c, u_d in ((u12a if s == 0 else u12b, 0, u1_d), (u12a if s == 0 else u12b, 1, u2_d), (u3, s, u3_d)):
                    loads.append((dst[:, :, c * D:(c + 1) * D], u_d[s, :, :].rearrange("(k p) n -> p k n", p=P)))
            for dst, src in loads:
                sp.dma_start(dst, src).then_inc(s_wts, 16)
            assert 16 * len(loads) == WTS

            def adj_pair(sweep, q):
                for b in range(2):
                    if some(NP * sweep + q):
                        sp.wait_ge(s_adjf[b], NP * sweep + q)
                    if sweep == 0 and some(q):
                        sp.wait_ge(s_csum[b], q)
                    if sweep == 1 and isinstance(q, int):
                        sp.wait_ge(s_csum[b], NP)
                    sp.dma_start(adjb[:, b, :], adjt_d[bass.ds(2 * q + b, 1), :, :].rearrange("a p n -> p (a n)")
                                 ).then_inc(s_adj[b], 16)
                    if sweep == 1:
                        if isinstance(q, int):
                            sp.wait_ge(s_pust[b], 16 * NP)
                        sp.dma_start(pu2[:, b, :], pu2_d[bass.ds((2 * q + b) * P, P), :]).then_inc(s_puld[b], 16)

            adj_pair(0, 0)
            with sp.Fori(1, NP) as q:
                adj_pair(0, q)
            adj_pair(1, 0)
            with sp.Fori(1, NP) as q:
                adj_pair(1, q)
            sp.wait_ge(s_S, 2 * NT)
            sp.dma_start(x_again, x_d.rearrange("(t p) n -> p t n", p=P)).then_inc(s_x2, 16)
            with sp.Fori(0, NP) as q:
                adj_pair(2, q)

        @block.gpsimd
        def _(pool):
            pool.memset(ones[:, :], 1.0).then_inc(s_ms, 1)
            pool.memset(half[:, :], -0.5).then_inc(s_ms, 1)
            for k in range(GEO):
                pool.memset(expo[:, :, k:k + 1], -0.5 ** (k + 1)).then_inc(s_ms, 1)
            pool.memset(cacc[:, :, :], 0.0).then_inc(s_pool, 1)
            pool.wait_ge(s_ms, 2 + GEO)

            def past_waits():
                pool.nop().then_inc(s_pgo, 1)

            def rsqrt_guess(n):
                pool.wait_ge(s_var, n + 1)
                pool.tensor_tensor(rstd[:, :], tn[:, :], half[:, :], ALU.pow).then_inc(s_pow, 1)

            def steps(q):
                pool.wait_ge(s_low, q + 1)
                pool.tensor_tensor(step[:, :, :], low0[:, :].rearrange("p (b a) -> p b a", a=1).to_broadcast([P, G4, GEO]),
                                   expo[:, :, :], ALU.pow).then_inc(s_step, 1)

            def any_flag(t):
                pool.wait_ge(s_fl, t + 1)
                past_waits()
                pool.partition_all_reduce(flagi[:, :], flags[:, :], P, ADD).then_inc(s_fa, 1)

            def z_s(s, q, b):
                t = q * G4 + b
                zt = tile_of(z, t, 0, D)
                if s == 0:
                    blk = adjb[:, b % 2, :].rearrange("p (t h i) -> p t h i", h=2, i=P // 2)
                    pool.wait_ge(s_adj[b % 2], 16 * (2 * q + b // 2) + 16)
                    for h in range(2):
                        pool.wait_ge(s_pool, 2 * t + h + 1)
                        pool.tensor_tensor(cacc[:, :, :], cacc[:, :, :], blk[:, :, h, :], ALU.add).then_inc(s_pool, 1)
                    pool.wait_ge(s_pool, 2 * t + 3)
                    pool.nop().then_inc(s_csum[b % 2], 1)
                    pool.wait_ge(s_pu0, t + 1)
                    if some(q):
                        pool.wait_ge(s_zst[b], 16 * q)
                    past_waits()
                    pool.tensor_tensor(zq[:, b, :], tz[:, 0, :], zt, ALU.add).then_inc(s_zs, 1)
                else:
                    pool.wait_ge(s_Se, NT + t + 1)
                    for h in range(2):
                        past_waits()
                        pool.tensor_tensor(zt, zt, tz[:, h, :], ALU.add).then_inc(s_zs, 1)
                        pool.wait_ge(s_zs, NT + 2 * t + h + 1)

            def z_a(s, t, b):
                if s == 0:
                    pool.wait_ge(s_AUa, t + 1)
                    pool.wait_ge(s_zs, t + 1)
                    pool.tensor_tensor(zq[:, b, :], zq[:, b, :], ta[:, :], ALU.add).then_inc(s_za, 1)
                    pool.wait_ge(s_za, t + 1)
                    pool.dma_start(zs_d[bass.ds(t * P, P), :], zq[:, b, :]).then_inc(s_zst[b], 16)
                else:
                    pool.wait_ge(s_Ae, NT + t + 1)
                    past_waits()
                    pool.tensor_tensor(tile_of(z, t, 0, D), tile_of(z, t, 0, D), ta[:, :], ALU.add).then_inc(s_za, 1)

            rsqrt_guess(0)
            for s in range(2):
                steps(s * NQ)

                def quad(q, more):
                    t0 = q * G4
                    for b in range(G4):
                        z_s(s, q, b)
                    for b in range(G4):
                        any_flag(s * NT + t0 + b)
                        if b == 1:
                            z_a(s, t0, 0)
                    z_a(s, t0 + 1, 1)
                    if more:
                        steps(s * NQ + q + 1)
                    for b in range(2, G4):
                        z_a(s, t0 + b, b)

                quads(pool, s, quad)
                if s == 0:
                    pool.wait_ge(s_A, NT)
                    pool.wait_ge(s_AU, NT)
                    pool.wait_ge(s_zs, NT)
                    for b in range(G4):
                        pool.wait_ge(s_zst[b], 16 * NQ)
                    pool.dma_start(z, zs_d.rearrange("(t p) n -> p t n", p=P)).then_inc(s_zld, 16)
                    for dst, src in [(wsg[:, :, 0:D], wsa_d.rearrange("(k p) n -> p k n", p=P)),
                                     (wsg[:, :, D:D + 4], wgate_d.rearrange("(k p) n -> p k n", p=P)),
                                     (wg, wg_d.rearrange("(k p) n -> p k n", p=P)),
                                     (asa, asa_d.partition_broadcast(P)), (bg, bg_d.partition_broadcast(P)),
                                     (bab[:, 0:1], ba_d.partition_broadcast(P)), (bab[:, 1:2], bb_d.partition_broadcast(P))]:
                        pool.dma_start(dst, src).then_inc(s_l1w, 16)
                    pool.wait_ge(s_zld, 16)
            rsqrt_guess(1)
            rsqrt_guess(2)

            pool.wait_ge(s_slc, 1)
            pool.wait_ge(s_me, NT)

            def scores(t, b):
                if some(t - 1):
                    pool.wait_ge(s_mk, t - 1)
                    past_waits()
                pool.tensor_tensor(sco[:, b, :].rearrange("p (t i) -> p t i", i=P),
                                   slb[:, bass.ds(t * P, P)].rearrange("p (a i) -> p a i", a=1).to_broadcast([P, NT, P]),
                                   sr[:, :].rearrange("p (t a) -> p t a", a=1).to_broadcast([P, NT, P]),
                                   ALU.add).then_inc(s_sco, 1)

            for b in range(2):
                scores(b, b)
            with pool.Fori(1, NP) as q:
                for b in range(2):
                    scores(2 * q + b, b)

        @block.scalar
        def _(act):
            act.wait_ge(s_x, 16)
            act.wait_ge(s_nrm, 1)
            for t in range(NT):
                act.activation(xc[:, t, 0:D], r3[:, t, 0:D], ACT.Relu, bias=nmr[:, t:t + 1],
                               scale=rstd[:, t:t + 1]).then_inc(s_xc, 1)
            act.wait_ge(s_w12p, 1)
            act.activation(w12[:, :, :], pS[:, 0:KD * P], ACT.Copy).then_inc(s_w12, 1)

            def xt_copies(s):
                for n in range(KD * NCH):
                    b = n % 2
                    act.wait_ge(s_tp[b], 4 * s + n // 2 + 1)
                    act.activation(xt[:, n % KD, (n // KD) * CH:(n // KD + 1) * CH], pT[b][:, :], ACT.Copy).then_inc(s_te[b], 1)

            def qk_high(s):
                for n in range(NCH):
                    for b, dst in ((0, qs), (1, kh)):
                        act.wait_ge(s_qp[b], NCH * s + n + 1)
                        act.activation(dst[:, n * CH:(n + 1) * CH], pT[b][:, :], ACT.Copy, scale=SQK).then_inc(s_qh[b], 1)

            def exps(t, b, first):
                act.wait_ge(s_max, t + 1)
                if not first:
                    act.wait_ge(s_em, t - G4 + 1)
                act.activation(ew[:, b, :], pL[:, :], ACT.Exp, bias=nbias[:, b:b + 1], scale=LSCALE,
                               accum_out=zsum[:, b:b + 1]).then_inc(s_e, 1)

            def s_tile(s, q, b):
                t = q * G4 + b
                if s == 0:
                    act.wait_ge(s_S, t + 1)
                    if some(t):
                        act.wait_ge(s_rinv, t)
                    act.activation(pst[:, :], pS[:, 0:D + 1], ACT.Copy).then_inc(s_Se, 1)
                    act.wait_ge(s_pt, t + 1)
                    act.activation(ptt, pS[:, 0:KD * P], ACT.Copy).then_inc(s_ptc, 1)
                    act.wait_ge(s_PU, t + 1)
                    act.wait_ge(s_rinv, t + 1)
                    rt = rinv[:, bass.ds(t, 1)]
                    if some(t):
                        act.wait_ge(s_zs, t)
                    act.activation(tz[:, 0, :], pT[0][:, 0:D], ACT.Copy, scale=rt).then_inc(s_pu0, 1)
                    if some(2 * q + b // 2):
                        act.wait_ge(s_pust[b % 2], 16 * (2 * q + b // 2))
                    act.activation(pu2[:, b % 2, :], pT[0][:, D:2 * D], ACT.Copy).then_inc(s_puc, 1)
                    act.activation(tile_of(g, t, 0, D), pT[1][:, 0:D], ACT.Copy, scale=rt)
                    act.activation(tile_of(g, t, D, 2 * D), pT[1][:, D:2 * D], ACT.Copy).then_inc(s_PUe, 1)
                    act.wait_ge(s_puc, t + 1)
                    act.dma_start(pu2_d[bass.ds(t * P, P), :], pu2[:, b % 2, :]).then_inc(s_pust[b % 2], 16)
                else:
                    act.wait_ge(s_S, NT + t + 1)
                    act.wait_ge(s_zs, NT + 2 * t)
                    act.activation(tz[:, 0, :], pS[:, 0:D], ACT.Copy, scale=rinv[:, bass.ds(t, 1)])
                    act.activation(tz[:, 1, :], pS[:, D:2 * D], ACT.Copy, scale=cinv[:, bass.ds(t, 1)]).then_inc(s_Se, 1)

            def a_tile(s, t, b, more):
                for q in range(NCH):
                    act.wait_ge(s_emu, NCH * (s * NT + t) + q + 1)
                    if q == 0 and some(s * NT + t):
                        act.wait_ge(s_A, s * NT + t)
                    act.activation(emt[:, 4 * q:4 * q + 4, :], pT[q % 2][:, :], ACT.Copy).then_inc(s_et, 1)
                if more and b < 2:
                    exps(s * NT + t + G4, b, False)
                act.wait_ge(s_A, s * NT + t + 1)
                act.wait_ge(s_dinv, s * NT + t + 1)
                if s == 0:
                    act.activation(xst[:, :], pA[:, 0:D], ACT.Copy, scale=dinv[:, b:b + 1]).then_inc(s_Ae, 1)
                    if more and b == 1:
                        exps(s * NT + t + G4 + 1, b + 1, False)
                    act.wait_ge(s_at, t + 1)
                    act.activation(xtt, pA[:, 0:KD * P], ACT.Copy).then_inc(s_atc, 1)
                    act.activation(xt[:, :, bass.ds(t * P, P)], pA[:, 0:KD * P].rearrange("p (k i) -> p k i", k=KD), ACT.Copy).then_inc(s_atc, 1)
                    act.wait_ge(s_AU, t + 1)
                    if some(t):
                        act.wait_ge(s_za, t)
                    act.activation(ta[:, :], pT[0][:, 0:D], ACT.Copy).then_inc(s_AUa, 1)
                    act.activation(tile_of(r3, t, 0, D), pT[0][:, D:2 * D], ACT.Copy).then_inc(s_AUe, 1)
                else:
                    act.wait_ge(s_za, NT + t)
                    act.activation(ta[:, :], pA[:, 0:D], ACT.Copy, scale=dinv[:, b:b + 1]).then_inc(s_Ae, 1)
                    if more and b == 1:
                        exps(s * NT + t + G4 + 1, b + 1, False)
                if more and b == 1:
                    exps(s * NT + t + G4 + 2, b + 2, False)

            for s in range(2):
                if s == 0:
                    xt_copies(s)
                qk_high(s)
                for b in range(G4):
                    exps(s * NT + b, b, s == 0)

                def quad(q, more):
                    t0 = q * G4
                    for b in range(G4):
                        s_tile(s, q, b)
                    for b in range(G4):
                        a_tile(s, t0 + b, b, more)

                quads(act, s, quad)

            act.wait_ge(s_nrm, 2)
            for t in range(NT):
                act.activation(r3[:, t, 0:D], z[:, t, :], ACT.Relu, bias=nmr[:, t:t + 1],
                               scale=rstd[:, t:t + 1]).then_inc(s_h1, 1)
            xt_copies(1)
            act.wait_ge(s_slb, NT)
            act.activation(slb[:, :], pL[:, :], ACT.Copy).then_inc(s_slc, 1)

            def edge_exp(t, b):
                act.wait_ge(s_lr, t + 1)
                act.activation(sco[:, b, :], sco[:, b, :], ACT.Exp, scale=-1.0).then_inc(s_ex, 1)

            def finish(t, b):
                act.wait_ge(s_gz, t + 1)
                act.activation(ge[:, :], gz[:, :], ACT.Exp, scale=-1.0).then_inc(s_ge, 1)
                act.wait_ge(s_y, t + 1)
                act.activation(fe[:, 0, :], fe[:, 1, :], ACT.Exp, scale=-1.0).then_inc(s_ye, 1)
                act.wait_ge(s_fin, t + 1)
                act.dma_start(out_d[bass.ds(t * P, P), :], fin[:, b, :]).then_inc(s_out[b], 16)

            edge_exp(0, 0)
            edge_exp(1, 1)
            finish(0, 0)
            with act.Fori(1, NP) as q:
                for b in range(2):
                    edge_exp(2 * q + b, b)
                    finish(2 * q + b - 1, 1 - b)
            finish(NT - 1, 1)
            for b in range(2):
                act.wait_ge(s_out[b], 16 * NP)

        @block.vector
        def _(dve):
            def chain_on(chain_sem):
                count = [0]

                def mark(ins):
                    count[0] += 1
                    ins.then_inc(chain_sem, 1)
                    return count[0]

                def done(n):
                    dve.wait_ge(chain_sem, n)

                def link(ins):
                    done(mark(ins))

                def fresh():
                    dve.sem_clear(chain_sem)
                    count[0] = 0

                return link, mark, done, fresh

            main = chain_on(s_dve)
            branch = chain_on(s_fb)
            link, fresh = main[0], main[3]

            def loop(first, last, body):
                dve.nop()
                fresh()
                with dve.Fori(first, last) as q:
                    body(q)
                    dve.nop()
                    fresh()

            def norm(n, src):
                for t in range(NT):
                    ins = dve.bn_stats(stats[:, t, :], src[:, t, 0:D])
                link(ins)
                for t in range(NT):
                    ins = dve.bn_aggr(mv[:, t, :], stats[:, t, :])
                link(ins)
                dve.tensor_scalar(tn[:, :], mv[:, :, 1], LN_EPS, None, ALU.add).then_inc(s_var, 1)
                dve.wait_ge(s_pow, n + 1)
                link(dve.tensor_tensor(nmr[:, :], rstd[:, :], rstd[:, :], ALU.mult))
                link(dve.tensor_tensor(nmr[:, :], nmr[:, :], tn[:, :], ALU.mult))
                link(dve.tensor_scalar(nmr[:, :], nmr[:, :], -0.5, 1.5, ALU.mult, ALU.add))
                link(dve.tensor_tensor(rstd[:, :], rstd[:, :], nmr[:, :], ALU.mult))
                link(dve.scalar_tensor_tensor(nmr[:, :], mv[:, :, 0], -1.0, rstd[:, :], ALU.mult, ALU.mult))

            dve.memset(xc[:, :, D:D + 1], 1.0).then_inc(s_col, 1)
            dve.memset(big8[:, :, :], BIG)
            dve.memset(again[:, :], 0.0)
            dve.memset(zero8[:, :], 0.0).then_inc(s_dms, 1)
            dve.wait_ge(s_x, 16)
            norm(0, r3)
            dve.nop().then_inc(s_nrm, 1)

            def qk_low(s):
                for n in range(NCH):
                    cols = slice(n * CH, (n + 1) * CH)
                    dve.wait_ge(s_qh[0], NCH * s + n + 1)
                    dve.scalar_tensor_tensor(qs[DA:P, cols], pT[0][DA:P, :], SQK, qs[DA:P, cols],
                                             ALU.mult, ALU.subtract).then_inc(s_qe[0], 1)
                    dve.wait_ge(s_qh[1], NCH * s + n + 1)
                    dve.scalar_tensor_tensor(kl[:, cols], pT[1][:, :], SQK, kh[:, cols],
                                             ALU.mult, ALU.subtract).then_inc(s_qe[1], 1)

            def row_max(t, b):
                dve.wait_ge(s_L, t + 1)
                link(dve.tensor_reduce(nmax[:, b:b + 1], pL[:, :], AX.X, ALU.max))
                dve.tensor_scalar(nbias[:, b:b + 1], nmax[:, b:b + 1], -LSCALE, None, ALU.mult).then_inc(s_max, 1)

            def along(buf, B, n):
                return buf[:, B].rearrange("p (b a) -> p b a", a=1).to_broadcast([P, B.stop - B.start, n])

            def probe(B, chain):
                link, mark, done, fresh = chain
                passes = []
                for b in range(B.start, B.stop):
                    if len(passes) >= 2:
                        done(passes[-2])
                    passes.append(mark(dve.scalar_tensor_tensor(junk[:, b % 2, :], ew[:, b, :], cur[:, b, 0:1], ew[:, b, :],
                                                                   ALU.is_ge, ALU.mult, accum_out=mass[:, b:b + 1])))
                done(passes[-1])
                link(dve.tensor_tensor(cur[:, B, 1], target[:, B], mass[:, B], ALU.subtract))
                dve.tensor_scalar(is_lo[:, B], cur[:, B, 1], 0.0, None, ALU.is_le)
                link(dve.tensor_scalar(is_hi[:, B], cur[:, B, 1], 0.0, None, ALU.is_gt))
                dve.copy_predicated(lo[:, B, :], along(is_lo, B, 2), cur[:, B, :])
                link(dve.copy_predicated(hi[:, B, :], along(is_hi, B, 2), cur[:, B, :]))

            def middle(B, chain):
                link, mark, done, fresh = chain
                link(dve.tensor_tensor(qa[:, B], lo[:, B, 0], hi[:, B, 0], ALU.add))
                link(dve.tensor_scalar(cur[:, B, 0], qa[:, B], 0.5, None, ALU.mult))

            def interpolate(s, B, chain):
                link, mark, done, fresh = chain
                link(dve.tensor_tensor(gap[:, B, :], hi[:, B, :], lo[:, B, :], ALU.subtract))
                dve.scalar_tensor_tensor(qa[:, B], lo[:, B, 0], AIM[s], lo[:, B, 1], ALU.mult, ALU.subtract)
                link(dve.reciprocal(qb[:, B], gap[:, B, 1]))
                link(dve.tensor_tensor(qa[:, B], qa[:, B], qb[:, B], ALU.mult))
                link(dve.scalar_tensor_tensor(qa[:, B], qa[:, B], CLIP, gap[:, B, 0], ALU.min, ALU.mult))
                link(dve.tensor_tensor(cur[:, B, 0], qa[:, B], lo[:, B, 0], ALU.add))

            def near_end(B, chain):
                link, mark, done, fresh = chain
                link(dve.scalar_tensor_tensor(is_hi[:, B], hi[:, B, 0], NEAR, hi[:, B, 1], ALU.mult, ALU.is_ge))
                link(dve.copy_predicated(cur[:, B, 0], is_hi[:, B], hi[:, B, 0]))

            def settle(last, B, chain):
                link, mark, done, fresh = chain
                read = []
                for b in range(B.start, B.stop):
                    if len(read) >= 2:
                        done(read[-2])
                    link(dve.scalar_tensor_tensor(em[:, b % 2, :], ew[:, b, :], last[:, b, 0:1], ew[:, b, :],
                                                  ALU.is_lt, ALU.mult, accum_out=mass[:, b:b + 1]))
                    read.append(mark(dve.max(top8[:, b, :], em[:, b % 2, :])))
                done(read[-1])
                link(dve.tensor_tensor(mass[:, B], zsum[:, B], mass[:, B], ALU.subtract))
                for b in range(B.start, B.stop):
                    ins = dve.tensor_tensor_scan(pre8[:, b, :], top8[:, b, :], zero8[:, :], mass[:, b:b + 1], ALU.add, ALU.add)
                link(ins)
                dve.tensor_tensor(short[:, B], pre8[:, B, 7], target[:, B], ALU.is_lt)
                link(dve.tensor_tensor(abv8[:, B, :], pre8[:, B, :], top8[:, B, :], ALU.subtract))
                link(dve.tensor_tensor(cut8[:, B, :], abv8[:, B, :], along(target, B, 8), ALU.is_ge))
                link(dve.copy_predicated(top8[:, B, :], cut8[:, B, :], big8[:, B, :]))
                link(dve.tensor_reduce(tf[:, B], top8[:, B, :], AX.X, ALU.min))
                dve.scalar_tensor_tensor(qb[:, B], tf[:, B], TOP, short[:, B], ALU.is_gt, ALU.max)
                link(dve.tensor_tensor(cut8[:, B, :], top8[:, B, :], along(tf, B, 8), ALU.not_equal))
                dve.tensor_copy(short[:, B], qb[:, B])
                link(dve.copy_predicated(abv8[:, B, :], cut8[:, B, :], big8[:, B, :]))
                link(dve.tensor_reduce(above[:, B], abv8[:, B, :], AX.X, ALU.min))
                dve.reciprocal(qb[:, B], tf[:, B])
                link(dve.tensor_tensor(qa[:, B], target[:, B], above[:, B], ALU.subtract))
                link(dve.tensor_tensor(qa[:, B], qa[:, B], qb[:, B], ALU.mult))
                link(dve.tensor_scalar(ties[:, B], qa[:, B], 1.0, None, ALU.add))

            def mask(b, chain):
                link, mark, done, fresh = chain
                link(dve.scalar_tensor_tensor(em[:, b % 2, :], ew[:, b, :], tf[:, b:b + 1], ew[:, b, :], ALU.is_ge, ALU.mult,
                                              accum_out=kept[:, b:b + 1]))

            def drop_ties(b, chain):
                link, mark, done, fresh = chain
                tie = junk[:, :, :].rearrange("p a n -> p (a n)").bitcast(F16)
                rank = ew[:, b, 0:N // 2].bitcast(F16)
                link(dve.tensor_scalar(tie, ew[:, b, :], tf[:, b:b + 1], None, ALU.is_equal))
                link(dve.tensor_tensor_scan(rank, tie, tie, 0.0, ALU.add, ALU.max))
                dve.tensor_scalar(qb[:, b:b + 1], tf[:, b:b + 1], -1.0, None, ALU.mult)
                link(dve.scalar_tensor_tensor(tie, rank, ties[:, b:b + 1], tie, ALU.is_ge, ALU.mult))
                link(dve.scalar_tensor_tensor(em[:, b % 2, :], tie, qb[:, b:b + 1], em[:, b % 2, :], ALU.mult, ALU.add,
                                              accum_out=kept[:, b:b + 1]))

            def narrow(n, b, chain):
                link, mark, done, fresh = chain
                B = slice(b, b + 1)

                def halve():
                    middle(B, chain)
                    probe(B, chain)

                if n <= 3:
                    for _ in range(n):
                        halve()
                else:
                    with dve.Fori(0, n):
                        halve()
                        dve.nop()
                        fresh()
                settle(hi, B, chain)
                mask(b, chain)

            def missing(b, chain):
                link, mark, done, fresh = chain
                B = slice(b, b + 1)
                link(dve.tensor_tensor(again[:, 0:1], kept[:, B], target[:, B], ALU.is_lt))
                link(dve.tensor_tensor(again[:, 0:1], again[:, 0:1], short[:, B], ALU.mult))
                link(dve.tensor_copy(is_lo[:, B], again[:, 0:1]))

            def retry(b, chain):
                link, mark, done, fresh = chain
                B = slice(b, b + 1)
                narrow(3, b, chain)
                missing(b, chain)
                link(dve.transpose(againt[:, :], again[:, :]))
                link(dve.tensor_reduce(anyr[:, :], againt[:, :], AX.X, ALU.max))
                total = sum(dve.value_load(anyr[p:p + 1, :], min_val=0, max_val=1) for p in range(0, P, 32))
                fresh()
                with dve.If(total):
                    narrow(HALVINGS, b, chain)
                    missing(b, chain)
                    dve.copy_predicated(above[:, B], is_lo[:, B], mass[:, B])
                    link(dve.copy_predicated(tf[:, B], is_lo[:, B], lo[:, B, 0]))
                    mask(b, chain)
                    fresh()
                link(dve.memset(flagi[0:1, 1:2], 1))
                fresh()

            def search(s, q):
                for b in range(G4):
                    dve.wait_ge(s_e, G4 * q + b + 1)
                link(dve.tensor_scalar(low0[:, :], zsum[:, :], FLOOR, None, ALU.mult))
                dve.nop().then_inc(s_low, 1)
                dve.tensor_scalar(target[:, :], zsum[:, :], P_NUC, None, ALU.mult)
                dve.tensor_copy(lo[:, :, 0], low0[:, :])
                dve.memset(hi[:, :, 0], TOP)
                link(dve.tensor_scalar(lo[:, :, 1], zsum[:, :], P_NUC - 1.0, None, ALU.mult))
                link(dve.tensor_copy(hi[:, :, 1], target[:, :]))
                dve.wait_ge(s_step, q + 1)
                B = slice(0, G4)
                for n, kind in enumerate(PROBES[s]):
                    if kind == "g":
                        link(dve.tensor_tensor(cur[:, :, 0], lo[:, :, 0], step[:, :, n], ALU.mult))
                    elif kind == "i":
                        interpolate(s, B, main)
                    else:
                        middle(B, main)
                    probe(B, main)
                    if s == 0 and 1 <= n <= G4:
                        t = G4 * q + n - 1
                        dve.wait_ge(s_Se, t + 1)
                        link(dve.tensor_scalar(den[:, :], pst[:, D:D + 1], 1e-12, None, ALU.max))
                        dve.reciprocal(rinv[:, bass.ds(t, 1)], den[:, :]).then_inc(s_rinv, 1)
                if some(q):
                    dve.wait_ge(s_emu, NCH * G4 * q)
                if s == 0:
                    interpolate(s, B, main)
                    near_end(B, main)
                    settle(cur, B, main)
                else:
                    settle(hi, B, main)

            def finish(t, b, more):
                if b >= 2:
                    dve.wait_ge(s_emu, NCH * (t - 1))
                mask(b, main)
                dve.tensor_tensor(flags[:, 0:1], kept[:, b:b + 1], target[:, b:b + 1], ALU.is_lt)
                link(dve.scalar_tensor_tensor(qa[:, b:b + 1], tf[:, b:b + 1], 0.999, target[:, b:b + 1], ALU.mult, ALU.add))
                dve.tensor_tensor(flags[:, 1:2], kept[:, b:b + 1], qa[:, b:b + 1], ALU.is_gt)
                link(dve.tensor_tensor(flags[:, 0:1], flags[:, 0:1], short[:, b:b + 1], ALU.mult))
                dve.nop().then_inc(s_fl, 1)
                if more and b > 0:
                    row_max(t + G4 - 1, b - 1)
                dve.wait_ge(s_fa, t + 1)
                dve.nop().then_inc(s_vgo, 1)
                unsettled = dve.value_load(flagi[0:1, 0:1], min_val=0, max_val=P)
                with dve.If(unsettled):
                    retry(b, branch)
                tied = dve.value_load(flagi[0:1, 1:2], min_val=0, max_val=P)
                with dve.If(tied):
                    drop_ties(b, branch)
                    branch[3]()
                dve.reciprocal(dinv[:, b:b + 1], kept[:, b:b + 1]).then_inc(s_dinv, 1)
                dve.wait_ge(s_dinv, t + 1)
                dve.nop().then_inc(s_em, 1)

            for s in range(2):
                qk_low(s)
                for b in range(G4):
                    row_max(s * NT + b, b)

                def quad(q, more=True):
                    search(s, s * NQ + q)
                    for b in range(G4):
                        finish(s * NT + G4 * q + b, b, more)
                    if more:
                        row_max(s * NT + G4 * q + 2 * G4 - 1, G4 - 1)

                if s == 0:
                    quad(0)
                loop(1 - s, NQ - 1, quad)
                quad(NQ - 1, False)
                if s == 0:
                    dve.wait_ge(s_pool, 2 * NT + 1)
                    dve.wait_ge(s_PUe, NT)
                    link(dve.tensor_reduce(cinv[:, :], cacc[:, :, :], AX.X, ALU.add))
                    link(dve.tensor_scalar(cinv[:, :], cinv[:, :], 1.0, 1e-12, ALU.add, ALU.max))
                    link(dve.reciprocal(cinv[:, :], cinv[:, :]))
                    dve.tensor_tensor(g[:, :, D:2 * D], g[:, :, D:2 * D],
                                      cinv[:, :].rearrange("p (t a) -> p t a", a=1).to_broadcast([P, NT, D]),
                                      ALU.mult).then_inc(s_gs, 1)

            dve.wait_ge(s_za, 2 * NT)
            norm(1, z)
            dve.wait_ge(s_x2, 16)
            for t in range(NT):
                ins = dve.tensor_scalar(z[:, t, :], z[:, t, :], rstd[:, t:t + 1], nmr[:, t:t + 1], ALU.mult, ALU.add)
            link(ins)
            link(dve.tensor_tensor(z[:, :, :], z[:, :, :], gamma[:, :].rearrange("p (a n) -> p a n", a=1).to_broadcast([P, NT, D]), ALU.mult))
            link(dve.tensor_tensor(z[:, :, :], z[:, :, :], beta[:, :].rearrange("p (a n) -> p a n", a=1).to_broadcast([P, NT, D]), ALU.add))
            link(dve.tensor_tensor(z[:, :, :], z[:, :, :], x_again, ALU.add))
            norm(2, z)
            dve.nop().then_inc(s_nrm, 1)
            dve.memset(h257[:, :, D:D + 1], 1.0).then_inc(s_col, 1)

            dve.wait_ge(s_l1w, WL1)
            for t in range(NT):
                dve.wait_ge(s_m, t + 1)
                dve.tensor_copy(h257[:, t, 0:D], pT[0][:, 0:D])
                dve.tensor_copy(xgate[:, t, D:D + 2], pT[0][:, D:D + 2])
                dve.tensor_copy(ga[:, t, :], pT[0][:, D + 2:D + 4])
                link(dve.tensor_copy(xgate[:, t, 0:D], pT[1][:, 0:D]))
                dve.scalar_tensor_tensor(w[:, 0:D], h257[:, t, 0:D], 1.0, asa[:, 0:D], ALU.mult, ALU.mult,
                                         accum_out=sl[:, t:t + 1])
                link(dve.scalar_tensor_tensor(w[:, D:2 * D], h257[:, t, 0:D], 1.0, asa[:, D:2 * D], ALU.mult, ALU.mult,
                                              accum_out=sr[:, t:t + 1]))
                dve.nop().then_inc(s_me, 1)
            for t in range(NT):
                if t >= 2:
                    dve.wait_ge(s_slb, t - 1)
                dve.tensor_scalar(emt[:, t % 2, :], ident[:, :], sl[:, t:t + 1], None, ALU.mult).then_inc(s_diag, 1)

            def leaky(t, b):
                dve.wait_ge(s_sco, t + 1)
                dve.scalar_tensor_tensor(sco[:, b, :], sco[:, b, :], 0.01, sco[:, b, :], ALU.mult, ALU.max).then_inc(s_lr, 1)

            def edges(t, q, b):
                dve.wait_ge(s_ex, t + 1)
                dve.wait_ge(s_adj[b], 16 * (2 * NP + q) + 16)
                if some(t - 1):
                    dve.wait_ge(s_xa, t - 1)
                dve.scalar_tensor_tensor(edge[:, b, :], adjb[:, b, :], 0.0, sco[:, b, :], ALU.not_equal, ALU.mult).then_inc(s_mk, 1)

            def output(t, q, b):
                pb, pa = (pS, pA) if b == 0 else (pT[0], pT[1])
                dve.wait_ge(s_xb, t + 1)
                if some(t):
                    dve.wait_ge(s_ge, t)
                link(dve.tensor_tensor(gz[:, :], pb[:, D:D + 2], tile_of(ga, t, 0, 2), ALU.add))
                dve.tensor_tensor(gz[:, :], gz[:, :], bab[:, :], ALU.add).then_inc(s_gz, 1)
                link(dve.tensor_tensor(fe[:, 1, :], pb[:, 0:D], bg[:, :], ALU.add))
                dve.wait_ge(s_ge, t + 1)
                link(dve.tensor_scalar(ge[:, :], ge[:, :], 1.0, None, ALU.add))
                link(dve.reciprocal(ge[:, :], ge[:, :]))
                dve.wait_ge(s_xa, t + 1)
                link(dve.tensor_scalar(den[:, :], pa[:, D:D + 1], 1e-5, None, ALU.add))
                link(dve.reciprocal(den[:, :], den[:, :]))
                link(dve.tensor_tensor(den[:, :], den[:, :], ge[:, 0:1], ALU.mult))
                link(dve.tensor_scalar(fe[:, 1, :], fe[:, 1, :], ge[:, 1:2], None, ALU.mult))
                dve.scalar_tensor_tensor(fe[:, 1, :], pa[:, 0:D], den[:, :], fe[:, 1, :], ALU.mult, ALU.add).then_inc(s_y, 1)
                dve.wait_ge(s_y, t + 1)
                dve.nop().then_inc(s_rd, 1)
                dve.wait_ge(s_ye, t + 1)
                link(dve.tensor_scalar(fe[:, 0, :], fe[:, 0, :], 1.0, None, ALU.add))
                link(dve.reciprocal(fe[:, 0, :], fe[:, 0, :]))
                if some(q):
                    dve.wait_ge(s_out[b], 16 * q)
                dve.tensor_tensor(fin[:, b, :], fe[:, 0, :], tile_of(z, t, 0, D), ALU.add).then_inc(s_fin, 1)

            leaky(0, 0)
            edges(0, 0, 0)
            leaky(1, 1)
            edges(1, 0, 1)
            leaky(2, 0)
            output(0, 0, 0)

            def l1_pair(q, more=True):
                edges(2 * q, q, 0)
                leaky(2 * q + 1, 1)
                output(2 * q - 1, q - 1, 1)
                edges(2 * q + 1, q, 1)
                if more:
                    leaky(2 * q + 2, 0)
                output(2 * q, q, 0)

            loop(1, NP - 1, l1_pair)
            l1_pair(NP - 1, False)
            output(NT - 1, NP - 1, 1)

        @block.tensor
        def _(pe):
            def mm(out, lhs, rhs, k, n):
                return pe.matmul(out, lhs, rhs, start=(k == 0), stop=(k == n - 1))

            pe.wait_ge(s_wts, WTS)
            for k in range(KD):
                ins = mm(pS[:, k * P:(k + 1) * P], w1t[:, k * P:(k + 1) * P], w22[:, :], 0, 1)
            ins.then_inc(s_w12p, 1)

            def x_transposes(s, src, ready):
                for n in range(KD * NCH):
                    k, c, b = n % KD, n // KD, n % 2
                    pe.wait_ge(ready, 4 * c + 4)
                    if n >= 2 or s > 0:
                        pe.wait_ge(s_te[b], 4 * s + n // 2)
                    for m in range(4):
                        ins = pe.transpose(pT[b][:, m * P:(m + 1) * P], src[:, 4 * c + m, k * P:(k + 1) * P], ident[:, :])
                    ins.then_inc(s_tp[b], 1)

            def qk(s):
                for n in range(NCH):
                    for b, wt in ((0, w12), (1, w33)):
                        if n > 0 or s > 0:
                            pe.wait_ge(s_qe[b], NCH * s + n)
                        if n == 0 and s == 0:
                            pe.wait_ge(s_te[b], 4)
                        if n == 0 and s > 0:
                            pe.wait_ge(s_AUe, NT)
                        for k in range(KD):
                            ins = mm(pT[b][:, :], wt[:, k, :], xt[:, k, n * CH:(n + 1) * CH], k, KD)
                        ins.then_inc(s_qp[b], 1)

            def logits(s, t):
                if some(s * NT + t):
                    pe.wait_ge(s_e, s * NT + t)
                for n in range(NCH):
                    cols = slice(n * CH, (n + 1) * CH)
                    mm(pL[:, cols], qs[:, bass.ds(t * P, P)], kh[:, cols], 0, 2)
                    ins = mm(pL[:, cols], qs[:, bass.ds(t * P, P)], kl[:, cols], 1, 2)
                ins.then_inc(s_L, 1)

            def s_tile(s, q, b):
                t = q * G4 + b
                pe.wait_ge(s_adj[b % 2], 16 * (s * NP + 2 * q + b // 2) + 16)
                if s == 0:
                    if some(t):
                        pe.wait_ge(s_ptc, t)
                    for j in range(NT):
                        mm(pS[:, 0:D + 1], adjb[:, b % 2, j * P:(j + 1) * P], xc[:, j, 0:D + 1], j, NT + 1)
                    mm(pS[:, 0:D + 1], ident[:, :], tile_of(xc, t, 0, D + 1), NT, NT + 1).then_inc(s_S, 1)
                else:
                    pe.wait_ge(s_Se, NT + t)
                    for j in range(NT):
                        mm(pS[:, :], adjb[:, b % 2, j * P:(j + 1) * P], g[:, j, :], j, NT + 2)
                    pe.wait_ge(s_puld[b % 2], 16 * (2 * q + b // 2) + 16)
                    mm(pS[:, D:2 * D], ident[:, :], pu2[:, b % 2, :], NT, NT + 2)
                    mm(pS[:, :], ident[:, :], tile_of(g, t, 0, 2 * D), NT + 1, NT + 2).then_inc(s_S, 1)
                pe.wait_ge(s_S, s * NT + t + 1)
                pe.nop().then_inc(s_adjf[b % 2], 1)
                if s == 0:
                    pe.wait_ge(s_Se, t + 1)
                    for k in range(KD):
                        ins = pe.transpose(pS[:, k * P:(k + 1) * P], pst[:, k * P:(k + 1) * P], ident[:, :])
                    ins.then_inc(s_pt, 1)
                    pe.wait_ge(s_ptc, t + 1)
                    if some(t):
                        pe.wait_ge(s_PUe, t)
                    for k in range(KD):
                        mm(pT[0][:, :], ptt[:, k, :], u12a[:, k, :], k, KD)
                    for k in range(KD):
                        ins = mm(pT[1][:, :], ptt[:, k, :], u12b[:, k, :], k, KD)
                    ins.then_inc(s_PU, 1)

            def a_tile(s, t, b, more):
                pe.wait_ge(s_em, s * NT + t + 1)
                if s == 0 and b > 0:
                    pe.wait_ge(s_AUe, t)
                for c in range(NCH):
                    if c >= 2:
                        pe.wait_ge(s_et, NCH * (s * NT + t) + c - 1)
                    elif s > 0:
                        pe.wait_ge(s_et, NCH * (s * NT + t))
                    for m in range(4):
                        col = (4 * c + m) * P
                        ins = pe.transpose(pT[c % 2][:, m * P:(m + 1) * P], em[:, b % 2, col:col + P], ident[:, :])
                    ins.then_inc(s_emu, 1)
                if more and b == 1:
                    logits(s, t + G4 + 1)
                if s == 1:
                    pe.wait_ge(s_Ae, NT + t)
                elif some(t):
                    pe.wait_ge(s_atc, 2 * t)
                for j in range(NT):
                    if j % 4 == 0:
                        pe.wait_ge(s_et, NCH * (s * NT + t) + j // 4 + 1)
                    ins = mm(pA[:, 0:D], emt[:, j, :], (xc if s == 0 else r3)[:, j, 0:D], j, NT)
                ins.then_inc(s_A, 1)
                if more and b < 2:
                    logits(s, t + G4 + 1 + b)
                if s == 0:
                    pe.wait_ge(s_Ae, t + 1)
                    for k in range(KD):
                        ins = pe.transpose(pA[:, k * P:(k + 1) * P], xst[:, k * P:(k + 1) * P], ident[:, :])
                    ins.then_inc(s_at, 1)
                    pe.wait_ge(s_atc, 2 * t + 1)
                    for k in range(KD):
                        ins = mm(pT[0][:, :], xtt[:, k, :], u3[:, k, :], k, KD)
                    ins.then_inc(s_AU, 1)

            for s in range(2):
                if s == 0:
                    pe.wait_ge(s_col, 1)
                    x_transposes(0, xc, s_xc)
                    for b in range(2):
                        pe.wait_ge(s_te[b], 4)
                    pe.wait_ge(s_w12, 1)
                qk(s)
                for b in range(2):
                    pe.wait_ge(s_qe[b], NCH * (s + 1))
                for b in range(G4):
                    logits(s, b)
                if s == 1:
                    pe.wait_ge(s_gs, 1)

                def quad(q, more):
                    t0 = q * G4
                    for b in range(G4):
                        s_tile(s, q, b)
                    if s == 0:
                        pe.wait_ge(s_PUe, t0 + G4)
                    if more:
                        logits(s, t0 + G4)
                    for b in range(G4):
                        a_tile(s, t0 + b, b, more)
                    if s == 0:
                        pe.wait_ge(s_AUe, t0 + G4)

                quads(pe, s, quad)

            x_transposes(1, r3, s_h1)
            for b in range(2):
                pe.wait_ge(s_te[b], 8)
            pe.wait_ge(s_l1w, WL1)
            for t in range(NT):
                if t >= 1:
                    pe.wait_ge(s_me, t)
                for k in range(KD):
                    mm(pT[0][:, 0:D + 4], xt[:, k, t * P:(t + 1) * P], wsg[:, k, :], k, KD)
                for k in range(KD):
                    ins = mm(pT[1][:, 0:D], xt[:, k, t * P:(t + 1) * P], wg[:, k, :], k, KD)
                ins.then_inc(s_m, 1)
            pe.wait_ge(s_me, NT)
            pe.wait_ge(s_col, 2)
            pe.wait_ge(s_ms, 2)
            for t in range(NT):
                pe.wait_ge(s_diag, t + 1)
                mm(pL[:, t * P:(t + 1) * P], ones[:, :], emt[:, t % 2, :], 0, 1).then_inc(s_slb, 1)

            def l1_pair(q):
                for b in range(2):
                    t = 2 * q + b
                    pb, pa = (pS, pA) if b == 0 else (pT[0], pT[1])
                    pe.wait_ge(s_adj[b], 16 * (2 * NP + q) + 16)
                    if some(t - 1):
                        pe.wait_ge(s_rd, t - 1)
                    for j in range(NT):
                        ins = mm(pb[:, 0:D + 2], adjb[:, b, j * P:(j + 1) * P], xgate[:, j, 0:D + 2], j, NT)
                    ins.then_inc(s_xb, 1)
                    pe.wait_ge(s_mk, t + 1)
                    for j in range(NT):
                        ins = mm(pa[:, 0:D + 1], edge[:, b, j * P:(j + 1) * P], h257[:, j, :], j, NT)
                    ins.then_inc(s_xa, 1)
                    pe.wait_ge(s_xb, t + 1)
                    pe.nop().then_inc(s_adjf[b], 1)

            l1_pair(0)
            with pe.Fori(1, NP) as q:
                l1_pair(q)

    return nc


_IDENT = np.eye(128, dtype=np.float32)


def kernel(x, adj, L0_gnn_W1, L0_gnn_W2, L0_gnn_W3, L0_gnn_U1, L0_gnn_U2, L0_gnn_U3, L0_gnn_gamma, L0_gnn_beta,
           L1_gnn_W_sa, L1_gnn_a_sa, L1_gnn_W_gcnb, L1_gnn_b_gcnb, L1_gnn_Wa, L1_gnn_ba, L1_gnn_Wb, L1_gnn_bb):
    import concourse.bacc as bacc
    from concourse.bass_utils import run_bass_kernel_spmd

    x = np.asarray(x)
    adj = np.asarray(adj)
    n, d = x.shape
    nt = n // 128
    wa, wb = np.asarray(L1_gnn_Wa), np.asarray(L1_gnn_Wb)
    arrays = {
        "x": x,
        "adjt": np.asarray(adj).reshape(nt, 128, nt, 128).transpose(0, 3, 2, 1).reshape(nt, 128, n),
        "w1t": np.asarray(L0_gnn_W1).T,
        "w2": L0_gnn_W2, "w3": L0_gnn_W3, "u1": L0_gnn_U1, "u2": L0_gnn_U2, "u3": L0_gnn_U3,
        "gamma": L0_gnn_gamma, "beta": L0_gnn_beta,
        "wsa": L1_gnn_W_sa, "asa": np.asarray(L1_gnn_a_sa).reshape(2 * d), "wg": L1_gnn_W_gcnb, "bg": L1_gnn_b_gcnb,
        "wgate": np.stack([wa[0, :d], wb[0, :d], wa[0, d:], wb[0, d:]], axis=1),
        "ba": L1_gnn_ba, "bb": L1_gnn_bb, "ident": _IDENT,
    }
    arrays = {k: np.ascontiguousarray(np.asarray(v)) for k, v in arrays.items()}
    nc = bacc.Bacc("TRN2", target_bir_lowering=False, num_devices=1)
    args = [nc.dram_tensor(f"in_{k}", v.shape, mybir.dt.from_np(v.dtype), kind="ExternalInput").ap() for k, v in arrays.items()]
    pu2 = nc.dram_tensor("pu2_spill", (n, d), mybir.dt.float32, kind="Internal").ap()
    zs = nc.dram_tensor("z_spill", (n, d), mybir.dt.float32, kind="Internal").ap()
    out = nc.dram_tensor("out_x", (n, d), mybir.dt.float32, kind="ExternalOutput").ap()
    gnn_block_program(nc, *args, pu2, zs, out)
    r = run_bass_kernel_spmd(nc, [{f"in_{k}": v for k, v in arrays.items()}], core_ids=[0])
    return r.results[0]["out_x"]
```
